# Optimizing a Trainium2 kernel written in Bass

```python
import numpy as np
import jax
import jax.numpy as jnp

def _softmax(x, axis=-1):
    return jax.nn.softmax(x, axis=axis)

def _gelu(x):
    return jax.nn.gelu(x, approximate=True)

def _silu(x):
    return jax.nn.silu(x)

def _sigmoid(x):
    return jax.nn.sigmoid(x)

def _layernorm(x, axis=-1, eps=1e-05):
    m = jnp.mean(x, axis=axis, keepdims=True)
    v = jnp.var(x, axis=axis, keepdims=True)
    return (x - m) / jnp.sqrt(v + eps)

def _scatter_add(tgt, idx, src, axis=0):
    return tgt.at[idx].add(src)

def _segment_sum(src, seg, n):
    return jax.ops.segment_sum(src, seg, n)
kernel_name = 'mk_seq_postln_d1_jaxref_r8_0238e1'

def setup_inputs(seed: int=0):
    np.random.seed(seed)
    _w = jnp.asarray

    def _L0_attn_setup():
        import jax, jax.numpy as jnp
        import numpy as np
        NUM_HEADS = 16

        def _sinusoid_rel_pos(seq_len, dim):
            pos = jnp.arange(seq_len - 1, -1, -1, dtype=jnp.float32)
            inv_freq = 1.0 / 10000.0 ** (jnp.arange(0, dim, 2, dtype=jnp.float32) / dim)
            ang = pos[:, None] * inv_freq[None, :]
            return jnp.concatenate([jnp.sin(ang), jnp.cos(ang)], axis=-1)

        def _rel_shift(x):
            B, H, S, L = x.shape
            x = jnp.pad(x, ((0, 0), (0, 0), (0, 0), (1, 0)))
            x = x.reshape(B, H, L + 1, S)
            return x[:, :, 1:S + 1, :]
        key = jax.random.key(seed)
        ks = jax.random.split(key, 8)
        B, S, C = (2, 256, 128)
        Dk, Dv, H = (128, 128, NUM_HEADS)
        dk = Dk // H
        scale = 0.02
        return {'x': jax.random.normal(ks[0], (B, S, C), dtype=jnp.float32), 'Wq': jax.random.normal(ks[1], (C, Dk), dtype=jnp.float32) * scale, 'Wk': jax.random.normal(ks[2], (C, Dk), dtype=jnp.float32) * scale, 'Wv': jax.random.normal(ks[3], (C, Dv), dtype=jnp.float32) * scale, 'u': jax.random.normal(ks[4], (H, dk), dtype=jnp.float32) * scale, 'v': jax.random.normal(ks[5], (H, dk), dtype=jnp.float32) * scale, 'Wo': jax.random.normal(ks[6], (Dv, C), dtype=jnp.float32) * scale, 'bo': jnp.zeros((C,), dtype=jnp.float32)}
    _L0_attn_in = _L0_attn_setup()

    def _L0_ffn_setup():
        import jax, jax.numpy as jnp
        import numpy as np
        TOP_K = 2
        NUM_EXPERTS = 8
        B, T, H, F = (4, 256, 128, 512)
        key = jax.random.key(seed)
        ks = jax.random.split(key, 6)
        s_in = 1.0 / np.sqrt(H)
        s_ff = 1.0 / np.sqrt(F)
        return {'x': jax.random.normal(ks[0], (B, T, H), dtype=jnp.float32), 'router_w': jax.random.normal(ks[1], (NUM_EXPERTS, H), dtype=jnp.float32) * s_in, 'router_b': jax.random.normal(ks[2], (NUM_EXPERTS,), dtype=jnp.float32) * 0.01, 'gate_w': jax.random.normal(ks[3], (NUM_EXPERTS, F, H), dtype=jnp.float32) * s_in, 'up_w': jax.random.normal(ks[4], (NUM_EXPERTS, F, H), dtype=jnp.float32) * s_in, 'down_w': jax.random.normal(ks[5], (NUM_EXPERTS, H, F), dtype=jnp.float32) * s_ff}
    _L0_ffn_in = _L0_ffn_setup()
    _d = {'L0_attn_x': _L0_attn_in['x'], 'L0_attn_Wq': _L0_attn_in['Wq'], 'L0_attn_Wk': _L0_attn_in['Wk'], 'L0_attn_Wv': _L0_attn_in['Wv'], 'L0_attn_u': _L0_attn_in['u'], 'L0_attn_v': _L0_attn_in['v'], 'L0_attn_Wo': _L0_attn_in['Wo'], 'L0_attn_bo': _L0_attn_in['bo'], 'L0_ffn_router_w': _L0_ffn_in['router_w'], 'L0_ffn_router_b': _L0_ffn_in['router_b'], 'L0_ffn_gate_w': _L0_ffn_in['gate_w'], 'L0_ffn_up_w': _L0_ffn_in['up_w'], 'L0_ffn_down_w': _L0_ffn_in['down_w']}
    _x0 = _d['L0_attn_x']
    _d['L0_attn_x'] = jax.random.normal(jax.random.fold_in(jax.random.key(seed), 1), (1, 2048, 128), dtype=_x0.dtype)
    del _x0
    return _d

def reference(L0_attn_x, L0_attn_Wq, L0_attn_Wk, L0_attn_Wv, L0_attn_u, L0_attn_v, L0_attn_Wo, L0_attn_bo, L0_ffn_router_w, L0_ffn_router_b, L0_ffn_gate_w, L0_ffn_up_w, L0_ffn_down_w):

    def _L0_attn_ref(x, Wq, Wk, Wv, u, v, Wo, bo):
        import jax, jax.numpy as jnp
        import numpy as np
        NUM_HEADS = 16

        def _sinusoid_rel_pos(seq_len, dim):
            pos = jnp.arange(seq_len - 1, -1, -1, dtype=jnp.float32)
            inv_freq = 1.0 / 10000.0 ** (jnp.arange(0, dim, 2, dtype=jnp.float32) / dim)
            ang = pos[:, None] * inv_freq[None, :]
            return jnp.concatenate([jnp.sin(ang), jnp.cos(ang)], axis=-1)

        def _rel_shift(x):
            B, H, S, L = x.shape
            x = jnp.pad(x, ((0, 0), (0, 0), (0, 0), (1, 0)))
            x = x.reshape(B, H, L + 1, S)
            return x[:, :, 1:S + 1, :]
        B, S, C = x.shape
        H = NUM_HEADS
        dk = Wq.shape[1] // H
        dv = Wv.shape[1] // H
        Q = (x @ Wq).reshape(B, S, H, dk).transpose(0, 2, 1, 3)
        K = (x @ Wk).reshape(B, S, H, dk).transpose(0, 2, 1, 3)
        V = (x @ Wv).reshape(B, S, H, dv).transpose(0, 2, 1, 3)
        r = _sinusoid_rel_pos(S, dk)
        term1 = jnp.einsum('bhqd,bhkd->bhqk', Q, K)
        term2 = jnp.einsum('bhqd,kd->bhqk', Q, r)
        term3 = jnp.einsum('hd,bhkd->bhk', u, K)[:, :, None, :]
        term4 = jnp.einsum('hd,kd->hk', v, r)[None, :, None, :]
        scores = (term1 + term3 + _rel_shift(term2 + term4)) / jnp.sqrt(jnp.asarray(dk, dtype=x.dtype))
        attn = jax.nn.softmax(scores, axis=-1)
        out = jnp.einsum('bhqk,bhkd->bqhd', attn, V).reshape(B, S, H * dv)
        return out @ Wo + bo

    def _L0_ffn_ref(x, router_w, router_b, gate_w, up_w, down_w):
        import jax, jax.numpy as jnp
        import numpy as np
        TOP_K = 2
        NUM_EXPERTS = 8
        B, T, H, F = (4, 256, 128, 512)
        logits = jnp.einsum('bth,eh->bte', x, router_w) + router_b
        topv, topi = jax.lax.top_k(logits, TOP_K)
        gates = jax.nn.softmax(topv, axis=-1)

        def body(acc, inputs):
            e, gw, uw, dw = inputs
            w = jnp.sum(gates * (topi == e), axis=-1)
            h = jax.nn.silu(jnp.einsum('bth,fh->btf', x, gw)) * jnp.einsum('bth,fh->btf', x, uw)
            y = jnp.einsum('btf,hf->bth', h, dw)
            return (acc + y * w[..., None], None)
        init = jnp.zeros_like(x)
        xs = (jnp.arange(NUM_EXPERTS), gate_w, up_w, down_w)
        out, _ = jax.lax.scan(body, init, xs)
        return out
    x = L0_attn_x
    x = _layernorm(x + _L0_attn_ref(x, L0_attn_Wq, L0_attn_Wk, L0_attn_Wv, L0_attn_u, L0_attn_v, L0_attn_Wo, L0_attn_bo), axis=-1)
    x = _layernorm(x + _L0_ffn_ref(x, L0_ffn_router_w, L0_ffn_router_b, L0_ffn_gate_w, L0_ffn_up_w, L0_ffn_down_w), axis=-1)
    return x

_drawn_inputs = setup_inputs


def setup_inputs(seed=0):
    import zlib

    import numpy as np

    out = dict(_drawn_inputs(seed))
    spreads = {'L0_attn_bo': (0.0, 0.1)}
    factors = {'L0_attn_Wq': 8.0,
     'L0_attn_Wk': 8.0,
     'L0_attn_Wv': 6.151,
     'L0_attn_u': 8.0,
     'L0_attn_v': 8.0,
     'L0_attn_Wo': 8.0}
    for name, (base, spread) in spreads.items():
        noise = np.random.default_rng([zlib.crc32(name.encode()), seed]).standard_normal(out[name].shape)
        drawn = base * np.exp(spread * noise) if base else spread * noise
        out[name] = jnp.asarray(drawn.astype(out[name].dtype))
    for name, factor in factors.items():
        out[name] = (out[name] * factor).astype(out[name].dtype)
    return out
```

```python
import concourse.bass as bass
from concourse import mybir
from concourse.alu_op_type import AluOpType as ALU
from contextlib import ExitStack
import numpy as np

S = 2048
C = 128
NH = 16
DK = C // NH
NE = 8
FF = 512
P = 128
T = S // P
BANK = 512
NC = S // BANK
TPC = BANK // P
NEG = -1.0e30
SCALE = float(DK) ** -0.5
EPS = 1e-5

Q_PARTS = [0, 1, 2, 0, 1, 0]
K_PARTS = [0, 0, 0, 1, 1, 2]
NP6 = len(Q_PARTS)
CONTENT = NP6 * DK
SCORE = 2 * CONTENT
CORNERS = T - 1
LOW_ROWS = SCORE + 3
UP_MAX_ROWS = SCORE + CORNERS
UP_ROWS = UP_MAX_ROWS + 3

TILES = NC * (T + 1)
PER_CHUNK = T + 1
PAIRS = 2 * T + 2
LEAD = 6
LAG = 3
PSLOTS = PER_CHUNK
M_OPS = 8
F_OPS = 4
LOADS = 18
LOOP_FIRST, LOOP_TURNS = 1, 4


def head_items(h):
    items = []
    if h is None or h + 1 < NH:
        items += [("max", 1, j) for j in range(LEAD, PAIRS)]
    if h is None or h + 2 < NH:
        items += [("max", 2, j) for j in range(LEAD)]
    if h is None or h + 1 < NH:
        items.insert(PAIRS - LEAD + (2 if h is None or h + 2 < NH else 0), ("rows", 1, 0))
    if h is None or h > 0:
        items.insert(min(5, len(items)), ("result", -1, 0))
    return items


FIRST_ITEMS = [("max", 0, j) for j in range(PAIRS)] + [("rows", 0, 0)] + [("max", 1, j) for j in range(LEAD)]
LOOP_ITEMS = len(head_items(None))
RESULT_AT = head_items(None).index(("result", -1, 0))


def item_base(h):
    if isinstance(h, int):
        return len(FIRST_ITEMS) + sum(len(head_items(i)) for i in range(h))
    return (len(FIRST_ITEMS) + len(head_items(0)) - LOOP_ITEMS) + h * LOOP_ITEMS


class Head:

    def __init__(self, h, slot, nth, static):
        self.h, self.slot, self.nth, self.static = h, slot, nth, static

    def plus(self, n):
        s = self.slot + n
        return Head(self.h + n, s % 3, self.nth + s // 3, self.static)


def fixed(h):
    return Head(h, h % 3, h // 3, True)


def in_loop(i, s):
    return Head(i * 3 + s, s % 3, i + s // 3, False)


def build(nc, x_rows, x_cols, w_qkv, uv_cols, u_row, w_o, bo_row, router_cols, router_bias,
          gate_cols, up_cols, down_cols, rot_sin, rot_cos, k_low_const, k_up_const, q_up_const,
          mask_low4, mask_up, ident_b, ident_f, fold, last_token, expert_ids, expert_rows,
          q_scratch, r_scratch, k_scratch, out):
    f32, bf16, u32 = mybir.dt.float32, mybir.dt.bfloat16, mybir.dt.uint32
    ACT, AX = mybir.ActivationFunctionType, mybir.AxisListType
    ctx = ExitStack()
    with ctx:
        def sb(name, shape, dt=f32):
            return ctx.enter_context(nc.sbuf_tensor(name, shape, dt))

        def ps(name, cols):
            return ctx.enter_context(nc.psum_tensor(name, [P, cols], f32))

        def sem(name):
            return ctx.enter_context(nc.semaphore(name))

        s_ps = [ps(f"s_ps{i}", BANK) for i in range(2)]
        mx_ps = [ps(f"mx_ps{i}", 2 * BANK) for i in range(2)]
        pv_ps = [ps(f"pv_ps{i}", BANK) for i in range(2)]

        def link(eng, sem_, value):
            def f(ins, k):
                ins.then_inc(sem_, 1)
                eng.wait_ge(sem_, value + k)
            return f

        w_sb = sb("w_sb", [P, 4, C])
        uv = sb("uv", [P, 3])
        u_r = sb("u_r", [1, C])
        ones = sb("ones", [1, P])
        wo = sb("wo", [P, C])
        bo_r = sb("bo_r", [1, C])
        rw = sb("rw", [P, NE])
        rb_r = sb("rb_r", [1, NE])
        id_b = sb("id_b", [P, P], bf16)
        id_f = sb("id_f", [P, P])
        mk_low4 = sb("mk_low4", [P, BANK], bf16)
        mk_up = sb("mk_up", [P, P], bf16)
        fold_sb = sb("fold_sb", [P, DK + 1])
        last_sb = sb("last_sb", [P, 1])
        ids_sb = sb("ids_sb", [P, NE])

        attn = sb("attn", [P, T, C])
        pro = ExitStack()

        def sa(name, shape, dt=f32):
            return pro.enter_context(nc.sbuf_tensor(name, shape, dt))

        q_low = [sa(f"q_low{i}", [LOW_ROWS, S], bf16) for i in range(3)]
        k_low = [sa(f"k_low{i}", [LOW_ROWS, S], bf16) for i in range(3)]
        q_up = [sa(f"q_up{i}", [UP_ROWS, S], bf16) for i in range(3)]
        k_up = [sa(f"k_up{i}", [UP_ROWS, S], bf16) for i in range(3)]
        v_head = [sa(f"v_head{i}", [P, T, 32]) for i in range(3)]
        probs = sa("probs", [P, PSLOTS, BANK])
        o_part = sa("o_part", [P, S])
        proj = sa("proj", [P, T, 4, C])
        s_next = sa("s_next", [P, NH, T])
        red = sa("red", [P, 3, T, 2])
        red_d = sa("red_d", [P, 3, T])
        m_a = sa("m_a", [P, 3, T])
        m_b = sa("m_b", [P, 3, T])
        m_max = sa("m_max", [P, 3, T])
        m_rest = sa("m_rest", [P, 3, T])
        m_parts = sa("m_parts", [P, 3, 3, T], bf16)
        m_rows = sa("m_rows", [3 * T, 3, P], bf16)
        d_next = sa("d_next", [P, 3, T])
        p_next = sa("p_next", [P, 3, T])
        f_next = sa("f_next", [P, T, DK])
        f_den = sa("f_den", [P, T])
        f_rden = sa("f_rden", [P, T])
        f_num = sa("f_num", [P, T, DK])
        tiles_seen = sem("tiles_seen")
        s_full, s_read = sem("s_full"), sem("s_read")
        p_free, picked = sem("p_free"), sem("picked")
        mx_full, mx_read = sem("mx_full"), sem("mx_read")
        o_read = sem("o_read")
        v_ready, next_ready = sem("v_ready"), sem("next_ready")
        rows_ready = sem("rows_ready")
        m_chain, f_chain = sem("m_chain"), sem("f_chain")
        stacked = [sem(f"stacked{i}") for i in range(3)]
        m_placed = [sem(f"m_placed{i}") for i in range(3)]
        consts = sem("consts")
        w_in, tab_in, later_in = sem("w_in"), sem("tab_in"), sem("later_in")
        pads, filled = sem("pads"), sem("filled")
        q_full, k_full, row_full = sem("q_full"), sem("k_full"), sem("row_full")
        a_proj, a_hi, a_row = sem("a_proj"), sem("a_hi"), sem("a_row")
        g_rot, g_prod = sem("g_rot"), sem("g_prod")
        d_pro = sem("d_pro")
        kept = sem("kept")

        with pro, nc.Block() as block:
            def tmp(name, shape, dt=f32):
                return pro.enter_context(nc.sbuf_tensor(name, shape, dt))

            xt = tmp("xt", [P, S + 1])
            t_sin = tmp("t_sin", [P, S])
            t_cos = tmp("t_cos", [P, S])
            qu, qv, qs, kf = (probs[:, i * NC:(i + 1) * NC].rearrange("p c n -> p (c n)") for i in range(4))
            split = [tmp(f"split{i}", [P, 3, 2 * BANK], bf16) for i in range(3)]


            def max_tile(pe, hd, j, bank):
                s = hd.slot
                if j >= 2 * T:
                    for b in range(2):
                        nc.tensor.matmul(bank[:, b * BANK:(b + 1) * BANK], id_b[:], mk_low4[:],
                                         start=True, stop=True)
                        for i in range(TPC):
                            t = 8 * (j - 2 * T) + TPC * b + i
                            c0 = b * BANK + i * P
                            last = nc.tensor.matmul(bank[:, c0:c0 + P], q_low[s][0:SCORE, t * P:(t + 1) * P],
                                                    k_low[s][0:SCORE, t * P:(t + 1) * P],
                                                    start=False, stop=True, skip_group_check=True)
                    return last
                t, half = j // 2, j % 2
                for b in range(2):
                    kc = 2 * half + b
                    left = min(max(t - TPC * kc, 0), TPC) * P
                    o = b * BANK
                    k0 = kc * BANK
                    if left:
                        last = nc.tensor.matmul(bank[:, o:o + left], q_low[s][0:SCORE, t * P:(t + 1) * P],
                                                k_low[s][0:SCORE, k0:k0 + left], start=True, stop=True)
                    if left < BANK:
                        last = nc.tensor.matmul(bank[:, o + left:o + BANK],
                                                q_up[s][0:UP_MAX_ROWS, t * P:(t + 1) * P],
                                                k_up[s][0:UP_MAX_ROWS, k0 + left:k0 + BANK],
                                                start=True, stop=True)
                        if t // TPC == kc:
                            last = nc.tensor.matmul(bank[:, o + left:o + left + P], id_b[:], mk_up[:],
                                                    start=False, stop=True, skip_group_check=True)
                return last

            def pe_item(pe, hd, item, number, slot):
                kind, ahead, j = item
                of = hd.plus(ahead)
                bank = mx_ps[slot]
                if kind == "max" and j == 0:
                    pe.wait_ge(stacked[of.slot], (of.nth + 1) * (16 * LOADS))
                if kind == "rows":
                    pe.wait_ge(m_chain, (of.h + 1) * M_OPS)
                if kind == "result":
                    pe.wait_ge(o_read, (of.h + 1) * NC + 2)
                pe.wait_ge(mx_read, number + 1)
                if kind == "max":
                    last = max_tile(pe, of, j, bank)
                elif kind == "rows":
                    last = nc.tensor.matmul(bank[0:3 * T, 0:P],
                                            m_parts[:, of.slot].rearrange("p a t -> p (a t)"), id_b[:],
                                            start=True, stop=True)
                else:
                    for t in range(T):
                        last = nc.tensor.matmul(bank[:, t * (DK + 1):(t + 1) * (DK + 1)],
                                                o_part[:, t * P:(t + 1) * P], fold_sb[:],
                                                start=True, stop=True)
                last.then_inc(mx_full, 1)

            def pe_scores(pe, hd, n):
                s, (c, kb) = hd.slot, divmod(n, PER_CHUNK)
                if n == 0:
                    pe.wait_ge(m_placed[s], (hd.nth + 1) * 32)
                pe.wait_ge(s_read, hd.h * TILES + (n + NC - 1))
                bank = s_ps[n % 2]
                q0 = c * BANK
                if kb == T:
                    for i in range(TPC):
                        t = TPC * c + i
                        last = nc.tensor.matmul(bank[:, i * P:(i + 1) * P], k_low[s][0:LOW_ROWS, t * P:(t + 1) * P],
                                                q_low[s][0:LOW_ROWS, t * P:(t + 1) * P],
                                                start=True, stop=True)
                else:
                    up = min(max(kb - TPC * c + 1, 0), TPC) * P
                    if up:
                        last = nc.tensor.matmul(bank[:, 0:up], k_up[s][0:UP_ROWS, kb * P:(kb + 1) * P],
                                                q_up[s][0:UP_ROWS, q0:q0 + up], start=True, stop=True)
                    if up < BANK:
                        last = nc.tensor.matmul(bank[:, up:BANK], k_low[s][0:LOW_ROWS, kb * P:(kb + 1) * P],
                                                q_low[s][0:LOW_ROWS, q0 + up:q0 + BANK], start=True, stop=True)
                last.then_inc(s_full, 1)

            def pe_values(pe, hd, n):
                s, (c, kb) = hd.slot, divmod(n, PER_CHUNK)
                if n == 0:
                    pe.wait_ge(v_ready, hd.h + 1)
                if kb == 0:
                    pe.wait_ge(o_read, hd.h * NC + (c + 1))
                on_diagonal = kb == T or kb // TPC == c
                if on_diagonal:
                    i = TPC if kb == T else kb - TPC * c
                    pe.wait_ge(picked, hd.h * (NC * (TPC + 1)) + (c * (TPC + 1) + i + 1))
                else:
                    pe.wait_ge(s_read, hd.h * TILES + (n + NC + 1))
                bank, src = pv_ps[c % 2], probs[:, n % PER_CHUNK]
                if kb == T:
                    for i in range(TPC):
                        last = nc.tensor.matmul(bank[32 * i:32 * i + 32, i * P:(i + 1) * P],
                                                v_head[s][:, TPC * c + i, :], src[:, i * P:(i + 1) * P],
                                                start=False, stop=True, skip_group_check=True)
                else:
                    g = kb % 4
                    last = nc.tensor.matmul(bank[32 * g:32 * g + 32, :], v_head[s][:, kb, :], src,
                                            start=(kb < 4), stop=True, skip_group_check=True)
                last.then_inc(p_free, 1)

            def pe_head(pe, hd):
                items = head_items(hd.h if hd.static else None)
                base = item_base(hd.h)
                even = (item_base(hd.h) if hd.static else item_base(LOOP_FIRST)) % 2
                at = 0
                for n in range(TILES + LAG):
                    if n < TILES:
                        while at < len(items) and at * TILES < (n + 1) * len(items) and (
                                items[at][0] != "result" or n >= 2 * LAG + 3):
                            pe_item(pe, hd, items[at], base + at, (even + at) % 2)
                            at += 1
                        pe_scores(pe, hd, n)
                    if n >= LAG and (n - LAG) % PER_CHUNK == T:
                        pe_values(pe, hd, n - LAG)
                    elif n >= LAG and (n - LAG) % PER_CHUNK % 4 == 3:
                        for m in range(n - LAG - 3, n - LAG + 1):
                            pe_values(pe, hd, m)

            def dve_maximum(dve, of):
                s = of.slot
                seq = link(dve, m_chain, of.h * M_OPS)
                seq(nc.vector.tensor_tensor(m_a[:, s], red[:, s, :, 0], red[:, s, :, 1], ALU.max), 1)
                seq(nc.vector.tensor_tensor(m_b[:, s], m_a[:, s], red_d[:, s], ALU.max), 2)
                seq(nc.vector.tensor_tensor(m_max[:, s], m_b[:, s], s_next[:, of.h, :], ALU.max), 3)
                seq(nc.vector.tensor_scalar(m_parts[:, s, 0], m_max[:, s], -1.0, None, ALU.mult), 4)
                seq(nc.vector.scalar_tensor_tensor(out=m_rest[:, s], in0=m_max[:, s], scalar=-1.0,
                                                   in1=m_parts[:, s, 0], op0=ALU.mult, op1=ALU.subtract), 5)
                seq(nc.vector.tensor_copy(m_parts[:, s, 1], m_rest[:, s]), 6)
                seq(nc.vector.tensor_tensor(m_parts[:, s, 2], m_rest[:, s], m_parts[:, s, 1], ALU.subtract), 7)
                nc.vector.tensor_tensor(d_next[:, s], s_next[:, of.h, :], m_max[:, s],
                                        ALU.subtract).then_inc(m_chain, 1)

            def dve_item(dve, hd, item, number, slot):
                kind, ahead, j = item
                of = hd.plus(ahead)
                bank, s = mx_ps[slot], of.slot
                dve.wait_ge(mx_full, number + 1)
                if kind == "max" and j < 2 * T:
                    nc.vector.reduce_max(red[:, s, j // 2, j % 2:j % 2 + 1], bank[:, :],
                                         AX.X).then_inc(mx_read, 1)
                elif kind == "max":
                    t0 = 8 * (j - 2 * T)
                    nc.vector.reduce_max(red_d[:, s, t0:t0 + 8], bank.rearrange("p (t k) -> p t k", k=P),
                                         AX.X).then_inc(mx_read, 1)
                    if j == PAIRS - 1:
                        dve.wait_ge(mx_read, number + 3)
                        dve_maximum(dve, of)
                elif kind == "rows":
                    nc.vector.tensor_copy(m_rows[:, s], bank[0:3 * T, 0:P]).then_inc(mx_read, 1)
                else:
                    seq = link(dve, f_chain, of.h * F_OPS)
                    dve.wait_ge(next_ready, of.h + 1)
                    o = bank[:, 0:T * (DK + 1)].rearrange("p (t d) -> p t d", d=DK + 1)
                    pn = p_next[:, s]
                    seq(nc.vector.tensor_tensor(f_next[:], proj[:, :, 3, bass.ds(of.h * DK, DK)],
                                                pn.unsqueeze(2).to_broadcast([P, T, DK]), ALU.mult), 1)
                    seq(nc.vector.tensor_tensor(f_den[:], o[:, :, DK], pn, ALU.add), 2)
                    seq(nc.vector.reciprocal(f_rden[:], f_den[:]), 3)
                    ins = nc.vector.tensor_tensor(f_num[:], o[:, :, 0:DK], f_next[:], ALU.add)
                    ins.then_inc(mx_read, 1)
                    dve.wait_ge(mx_read, number + 3)
                    seq(nc.vector.tensor_tensor(attn[:, :, bass.ds(of.h * DK, DK)], f_num[:],
                                                f_rden[:].unsqueeze(2).to_broadcast([P, T, DK]), ALU.mult), 4)

            def dve_head(dve, hd):
                base = item_base(hd.h)
                even = (item_base(hd.h) if hd.static else item_base(LOOP_FIRST)) % 2
                for i, item in enumerate(head_items(hd.h if hd.static else None)):
                    dve_item(dve, hd, item, base + i, (even + i) % 2)

            def act_result(act, hd, c):
                act.wait_ge(p_free, hd.h * TILES + ((c + 1) * PER_CHUNK + PSLOTS))
                nc.scalar.activation(o_part[:, c * BANK:(c + 1) * BANK], pv_ps[c % 2][:],
                                     ACT.Copy).then_inc(o_read, 1)

            def act_next(act, of):
                act.wait_ge(m_chain, (of.h + 1) * M_OPS)
                nc.scalar.activation(p_next[:, of.slot], d_next[:, of.slot], ACT.Exp,
                                     scale=SCALE).then_inc(next_ready, 1)

            def act_head(act, hd):
                for n in range(TILES):
                    act.wait_ge(s_full, hd.h * TILES + (n + 1))
                    act.wait_ge(p_free, hd.h * TILES + (n + 1))
                    nc.scalar.activation(probs[:, n % PER_CHUNK], s_ps[n % 2][:], ACT.Exp,
                                         scale=SCALE).then_inc(s_read, 1)
                    c, i = divmod(n, PER_CHUNK)
                    if i == LAG + 2:
                        if c:
                            if c == 1 and not (hd.static and hd.h == 0):
                                act.wait_ge(mx_full, item_base(hd.h) + (RESULT_AT + 1 if not hd.static else
                                            head_items(hd.h).index(("result", -1, 0)) + 1))
                            act_result(act, hd, c - 1)
                        elif not (hd.static and hd.h == 0):
                            act_result(act, hd.plus(-1) if hd.static else Head(hd.h - 1, 0, 0, False), NC - 1)
                    if n == TILES - 2 and not (hd.static and hd.h + 1 >= NH):
                        act_next(act, hd.plus(1))

            def pool_values(pool, of):
                nc.gpsimd.tensor_copy(v_head[of.slot][:, :, 0:DK],
                                      proj[:, :, 1, bass.ds(of.h * DK, DK)]).then_inc(v_ready, 1)

            def pool_head(pool, hd):
                for c in range(NC):
                    for i in range(TPC + 1):
                        n = c * PER_CHUNK + (TPC * c + i if i < TPC else T)
                        pool.wait_ge(s_read, hd.h * TILES + (n + NC + 1))
                        pool.sem_inc(tiles_seen, 1)
                        if i < TPC:
                            v = probs[:, n % PER_CHUNK, i * P:(i + 1) * P]
                            nc.gpsimd.affine_select(out=v, in_=v, compare_op=ALU.is_ge, fill=0.0, base=-2,
                                                    pattern=[[-1, P]], channel_multiplier=1).then_inc(picked, 1)
                        else:
                            v = probs[:, n % PER_CHUNK, :].rearrange("p (t q) -> p t q", q=P)
                            nc.gpsimd.affine_select(out=v, in_=v, compare_op=ALU.is_ge, fill=0.0, base=0,
                                                    pattern=[[0, TPC], [1, P]],
                                                    channel_multiplier=-1).then_inc(picked, 1)
                        if c == 0 and i == 0 and not (hd.static and hd.h + 1 >= NH):
                            pool_values(pool, hd.plus(1))

            def stack(sp, of):
                s = of.slot

                def put(dst, row0, parts, src):
                    n = len(parts)
                    step = parts[1] - parts[0] if n > 1 else 1
                    a = src[of.h, parts[0]:parts[0] + 1]
                    if step == 0:
                        a = a.to_broadcast([n, DK, a.shape[2]])
                    else:
                        a = src[of.h, parts[0]:parts[0] + n]
                    sp.dma_start(dst[row0:row0 + n * DK, 0:a.shape[2]], a).then_inc(stacked[s], 16)

                for row, lo, n in ((0, 0, 3), (3, 3, 2), (5, 5, 1)):
                    qp, kp = Q_PARTS[lo:lo + n], K_PARTS[lo:lo + n]
                    put(k_low[s], row * DK, kp, k_scratch)
                    put(k_up[s], row * DK, kp, k_scratch)
                    put(q_low[s], row * DK, qp, q_scratch)
                    put(q_up[s], row * DK, qp, q_scratch)
                    put(q_low[s], CONTENT + row * DK, qp, r_scratch)
                    put(q_up[s], CONTENT + row * DK, qp, r_scratch[:, :, :, 1:S])

            def place_maximum(sp, of):
                s = of.slot
                sp.wait_ge(mx_read, item_of_rows(of) + 3)
                for dst, r0 in ((q_low[s], SCORE), (q_up[s], UP_MAX_ROWS)):
                    sp.dma_start(dst[r0:r0 + 3, :], m_rows[:, s]).then_inc(m_placed[s], 16)

            def item_of_rows(of):
                if of.static:
                    if of.h == 0:
                        return PAIRS
                    return item_base(of.h - 1) + head_items(of.h - 1).index(("rows", 1, 0))
                return item_base(of.h - 1) + head_items(None).index(("rows", 1, 0))

            def sp_head(sp, hd):
                if not (hd.static and hd.h + 2 >= NH):
                    if not (hd.static and hd.h == 0):
                        sp.wait_ge(s_full, hd.h * TILES)
                    stack(sp, hd.plus(2))
                if not (hd.static and hd.h + 1 >= NH):
                    place_maximum(sp, hd.plus(1))

            def all_heads(eng, step):
                for h in range(LOOP_FIRST):
                    step(eng, fixed(h))
                with eng.Fori(0, LOOP_TURNS) as i:
                    for s in range(LOOP_FIRST, LOOP_FIRST + 3):
                        step(eng, in_loop(i, s))
                for h in range(LOOP_FIRST + 3 * LOOP_TURNS, NH):
                    step(eng, fixed(h))


            def split_done(half, i):
                return (2 * half + 1) * 11 + 2 + 3 * (i + 1)

            @block.sync
            def _(sp):
                sp.dma_start(w_sb[:], w_qkv).then_inc(w_in, 16)
                sp.dma_start(uv[:], uv_cols).then_inc(w_in, 16)
                sp.dma_start(u_r[:], u_row).then_inc(w_in, 16)
                for c in range(NC):
                    sp.dma_start(xt[:, c * BANK:(c + 1) * BANK], x_cols[:, c * BANK:(c + 1) * BANK]).then_inc(w_in, 16)
                sp.dma_start(t_sin[:], rot_sin).then_inc(tab_in, 16)
                sp.dma_start(t_cos[:], rot_cos).then_inc(tab_in, 16)
                for dst, src in ((id_b, ident_b), (id_f, ident_f), (mk_low4, mask_low4), (mk_up, mask_up),
                                 (fold_sb, fold), (last_sb, last_token)):
                    sp.dma_start(dst[:], src).then_inc(consts, 16)
                for i in range(3):
                    sp.dma_start(k_low[i][CONTENT:LOW_ROWS, :], k_low_const).then_inc(consts, 16)
                    sp.dma_start(k_up[i][CONTENT:UP_ROWS, :], k_up_const).then_inc(consts, 16)
                    sp.dma_start(q_up[i][SCORE:UP_MAX_ROWS, :], q_up_const).then_inc(consts, 16)
                for dst, src in ((wo, w_o), (bo_r, bo_row), (rw, router_cols), (rb_r, router_bias),
                                 (ids_sb, expert_ids)):
                    sp.dma_start(dst[:], src).then_inc(later_in, 16)
                for half in range(2):
                    for i, dst in enumerate((q_scratch, r_scratch, k_scratch)):
                        sp.wait_ge(d_pro, split_done(half, i))
                        for part in range(3):
                            sp.dma_start(dst[:, part, :, half * 2 * BANK:(half + 1) * 2 * BANK],
                                         split[i][:, part]).then_inc(kept, 16)
                sp.wait_ge(kept, 18 * 16)
                sp.wait_ge(filled, 9)
                stack(sp, fixed(0))
                stack(sp, fixed(1))
                place_maximum(sp, fixed(0))
                all_heads(sp, sp_head)

            @block.tensor
            def _(pe):
                pe.sem_inc(p_free, PSLOTS)
                pe.sem_inc(mx_read, 2)
                pe.sem_inc(o_read, 2)
                pe.wait_ge(w_in, 7 * 16)
                pe.wait_ge(pads, 2)
                for c in range(NC):
                    cols = xt[:, c * BANK:(c + 1) * BANK]
                    if c >= 2:
                        pe.wait_ge(a_proj, 4 * (c - 1))
                    nc.tensor.matmul(mx_ps[c % 2][:, 0:BANK], w_sb[:, 0, :], cols, start=True, stop=True)
                    nc.tensor.matmul(mx_ps[c % 2][:, BANK:], w_sb[:, 1, :], cols,
                                     start=True, stop=True).then_inc(q_full, 1)
                    nc.tensor.matmul(s_ps[c % 2][:], w_sb[:, 2, :], cols, start=True, stop=True).then_inc(k_full, 1)
                    for t in range(TPC * c, TPC * (c + 1)):
                        if t >= 2:
                            pe.wait_ge(a_row, t - 1)
                        bank, here = pv_ps[t % 2], xt[:, t * P:(t + 1) * P]
                        nc.tensor.matmul(bank[:, 0:P], here, w_sb[:, 0, :], start=True, stop=False)
                        nc.tensor.matmul(bank[:, 0:P], ones[:], u_r[:], start=False, stop=True)
                        nc.tensor.matmul(bank[:, P:2 * P], here, w_sb[:, 3, :], start=True, stop=True)
                        nc.tensor.matmul(bank[:, 2 * P:], xt[:, t * P + 1:(t + 1) * P + 1],
                                         w_sb[:, 2:4, :].rearrange("p a c -> p (a c)"),
                                         start=True, stop=True).then_inc(row_full, 1)
                pe.wait_ge(consts, 15 * 16)
                pe.wait_ge(filled, 9)
                pe.wait_ge(a_proj, 4 * NC)
                pe.wait_ge(a_row, T)
                for i, item in enumerate(FIRST_ITEMS):
                    pe_item(pe, fixed(0), item, i, i % 2)
                all_heads(pe, pe_head)
                pe_item(pe, fixed(NH), ("result", -1, 0), item_base(NH), item_base(NH) % 2)

            @block.scalar
            def _(act):
                act.wait_ge(w_in, 7 * 16)
                for c in range(NC):
                    sl = slice(c * BANK, (c + 1) * BANK)
                    act.wait_ge(q_full, c + 1)
                    nc.scalar.activation(qv[:, sl], mx_ps[c % 2][:, 0:BANK], ACT.Identity,
                                         bias=uv[:, 1:2]).then_inc(a_proj, 1)
                    nc.scalar.activation(qs[:, sl], mx_ps[c % 2][:, BANK:], ACT.Identity,
                                         bias=uv[:, 2:3]).then_inc(a_proj, 1)
                    nc.scalar.activation(qu[:, sl], mx_ps[c % 2][:, 0:BANK], ACT.Identity,
                                         bias=uv[:, 0:1]).then_inc(a_proj, 1)
                    act.wait_ge(k_full, c + 1)
                    nc.scalar.activation(kf[:, sl], s_ps[c % 2][:], ACT.Copy).then_inc(a_proj, 1)
                    act.wait_ge(a_proj, 4 * (c + 1))
                    if c >= 2:
                        act.wait_ge(kept, 9 * 16)
                    o = (c % 2) * BANK
                    nc.scalar.activation(split[0][:, 0, o:o + BANK], qu[:, sl], ACT.Copy).then_inc(a_hi, 1)
                    nc.scalar.activation(split[2][:, 0, o:o + BANK], kf[:, sl], ACT.Copy).then_inc(a_hi, 1)
                    act.wait_ge(d_pro, c * 11 + 2)
                    nc.scalar.activation(split[1][:, 0, o:o + BANK], qv[:, sl], ACT.Copy).then_inc(a_hi, 1)
                    for t in range(TPC * c, TPC * (c + 1)):
                        act.wait_ge(row_full, t + 1)
                        nc.scalar.activation(proj[:, t].rearrange("p a c -> p (a c)"), pv_ps[t % 2][:],
                                             ACT.Copy).then_inc(a_row, 1)
                act.sem_inc(s_read, NC)
                act_next(act, fixed(0))
                all_heads(act, act_head)
                act_result(act, fixed(NH - 1), NC - 1)

            @block.vector
            def _(dve):
                nc.vector.memset(xt[:, S:S + 1], 0.0).then_inc(pads, 1)
                nc.vector.memset(ones[:], 1.0).then_inc(pads, 1)
                dve.wait_ge(tab_in, 32)
                seq = link(dve, d_pro, 0)
                k = 0
                for c in range(NC):
                    sl = slice(c * BANK, (c + 1) * BANK)
                    o = (c % 2) * BANK
                    dve.wait_ge(a_proj, 4 * c + 3)
                    seq(nc.vector.tensor_tensor(qv[:, sl], qv[:, sl], t_sin[:, sl], ALU.mult), k + 1)
                    dve.wait_ge(g_rot, c + 1)
                    seq(nc.vector.tensor_tensor(qv[:, sl], qv[:, sl], qs[:, sl], ALU.add), k + 2)
                    k += 2
                    for i, src in ((0, qu), (1, qv), (2, kf)):
                        dve.wait_ge(a_hi, 3 * (c + 1))
                        seq(nc.vector.tensor_tensor(src[:, sl], src[:, sl], split[i][:, 0, o:o + BANK], ALU.subtract), k + 1)
                        seq(nc.vector.tensor_copy(split[i][:, 1, o:o + BANK], src[:, sl]), k + 2)
                        seq(nc.vector.tensor_tensor(split[i][:, 2, o:o + BANK], src[:, sl],
                                                    split[i][:, 1, o:o + BANK], ALU.subtract), k + 3)
                        k += 3
                dve.wait_ge(g_prod, 1)
                seq(nc.vector.reduce_sum(s_next.rearrange("p h t -> p t h"),
                                         proj[:, :, 0, :].rearrange("p t (h d) -> p t h d", d=DK), AX.X), k + 1)
                seq(nc.vector.tensor_scalar(s_next[:, :, T - 1], s_next[:, :, T - 1], last_sb[:], None, ALU.add), k + 2)
                for i, item in enumerate(FIRST_ITEMS):
                    dve_item(dve, fixed(0), item, i, i % 2)
                all_heads(dve, dve_head)
                dve_item(dve, fixed(NH), ("result", -1, 0), item_base(NH), item_base(NH) % 2)

            @block.gpsimd
            def _(pool):
                for i in range(3):
                    nc.gpsimd.memset(v_head[i][:, :, DK:DK + 1], 1.0).then_inc(filled, 1)
                    nc.gpsimd.memset(v_head[i][:, :, DK + 1:], 0.0).then_inc(filled, 1)
                    nc.gpsimd.memset(q_up[i][0:SCORE, S - 1:S], 0.0).then_inc(filled, 1)
                pool.wait_ge(tab_in, 32)
                for c in range(NC):
                    sl = slice(c * BANK, (c + 1) * BANK)
                    pool.wait_ge(a_proj, 4 * c + 2)
                    nc.gpsimd.tensor_tensor(qs[:, sl], qs[:, sl], t_cos[:, sl], ALU.mult).then_inc(g_rot, 1)
                pool.wait_ge(a_row, T)
                nc.gpsimd.tensor_tensor(proj[:, :, 0, :], proj[:, :, 0, :], proj[:, :, 2, :],
                                        ALU.mult).then_inc(g_prod, 1)
                pool_values(pool, fixed(0))
                all_heads(pool, pool_head)

        with ExitStack() as late, nc.Block() as block:
            def tmp(name, shape, dt=f32):
                return late.enter_context(nc.sbuf_tensor(name, shape, dt))

            def sem_b(name):
                return late.enter_context(nc.semaphore(name))

            GROUPS = NC
            FB = FF // P
            TURNS = NE // 2
            x_in = tmp("x_in", [P, T, C])
            attn_t = tmp("attn_t", [P, S])
            y = tmp("y", [P, T, C])
            x1 = tmp("x1", [P, T, C])
            x1_t = tmp("x1_t", [P, S])
            stats = tmp("stats", [P, T, 6])
            mean_var = tmp("mean_var", [P, T, 2])
            std = tmp("std", [P, T])
            rstd = tmp("rstd", [P, T])
            logits = tmp("logits", [P, T, NE])
            top = tmp("top", [P, T, 8])
            top_id = tmp("top_id", [P, T, 8], u32)
            top_f = tmp("top_f", [P, T, 2])
            gap = tmp("gap", [P, T])
            e_gap = tmp("e_gap", [P, T])
            e_sum = tmp("e_sum", [P, T])
            gate = tmp("gate", [P, 2, T])
            pick = tmp("pick", [P, 2, T, NE])
            weight = tmp("weight", [P, T, NE])
            weight_t = tmp("weight_t", [NE, S])
            wg = [tmp(f"wg{i}", [P, FF]) for i in range(2)]
            wu = [tmp(f"wu{i}", [P, FF]) for i in range(2)]
            wd = [tmp(f"wd{i}", [P, FB, C]) for i in range(2)]
            row_of = [tmp(f"row_of{i}", [NE, P]) for i in range(2)]
            xw = tmp("xw", [P, S])
            sg = tmp("sg", [P, 2, BANK])
            hid = tmp("hid", [P, 2, BANK])
            zero_row = tmp("zero_row", [1, BANK])
            moe_t = tmp("moe_t", [P, S])
            res = tmp("res", [P, T, C])

            x_here, wload, turned = sem_b("x_here"), [sem_b(f"wload{i}") for i in range(2)], sem_b("turned")
            turned_a, turned_d = sem_b("turned_a"), sem_b("turned_d")
            projected, d_b, a_b = sem_b("projected"), sem_b("d_b"), sem_b("a_b")
            routed = sem_b("routed")
            x1_turned, x1_a, x1_d = sem_b("x1_turned"), sem_b("x1_a"), sem_b("x1_d")
            w_turned, w_read = sem_b("w_turned"), sem_b("w_read")
            g_full, silu_done, u_full = sem_b("g_full"), sem_b("silu_done"), sem_b("u_full")
            w_full, xw_done, hid_used = sem_b("w_full"), sem_b("xw_done"), sem_b("hid_used")
            zeroed = sem_b("zeroed")
            hid_done, y_full, y_kept = sem_b("hid_done"), sem_b("y_full"), sem_b("y_kept")
            y_turned, stored = sem_b("y_turned"), sem_b("stored")
            UNITS = GROUPS * FB
            y_bank = [mx_ps[c // 2][:, (c % 2) * BANK:(c % 2 + 1) * BANK] for c in range(NC)]
            o_bank = [s_ps[0], s_ps[1], pv_ps[0], pv_ps[1]]

            def norm(dve, seq, k, src, dst, wait_sqrt):
                for t in range(T):
                    nc.vector.bn_stats(stats[:, t], src[:, t]).then_inc(d_b, 1)
                k += T
                dve.wait_ge(d_b, k)
                for t in range(T):
                    nc.vector.bn_aggr(mean_var[:, t], stats[:, t]).then_inc(d_b, 1)
                k += T
                dve.wait_ge(d_b, k)
                seq(nc.vector.tensor_scalar(std[:], mean_var[:, :, 1], EPS, None, ALU.add), k + 1)
                dve.wait_ge(a_b, wait_sqrt)
                seq(nc.vector.reciprocal(rstd[:], std[:]), k + 2)
                k += 2
                for t in range(T):
                    nc.vector.tensor_scalar(dst[:, t], src[:, t], mean_var[:, t, 0:1], rstd[:, t:t + 1],
                                            ALU.subtract, ALU.mult).then_inc(d_b, 1)
                return k + T

            NORM = 3 * T + 2
            D_X1 = GROUPS + NORM
            D_ROUTE = D_X1 + 1 + 2 * T
            D_WEIGHT = D_ROUTE + 10

            @block.sync
            def _(sp):
                sp.dma_start(x_in[:], x_rows).then_inc(x_here, 16)

                def load(e, s):
                    for dst, src in ((wg[s], gate_cols), (wu[s], up_cols), (wd[s], down_cols),
                                     (row_of[s], expert_rows)):
                        sp.dma_start(dst[:], src[e]).then_inc(wload[s], 16)

                load(0, 0)
                load(1, 1)
                with sp.Fori(0, TURNS - 1) as i:
                    for s in range(2):
                        sp.wait_ge(hid_used, i * (2 * UNITS) + ((s + 1) * UNITS + 2))
                        load(i * 2 + (2 + s), s)
                for g in range(GROUPS):
                    sp.wait_ge(d_b, D_WEIGHT + GROUPS + 2 * T + 2 + TPC * (g + 1))
                    sp.dma_start(out.rearrange("b (t p) c -> p (b t) c", p=P)[:, g * TPC:(g + 1) * TPC],
                                 res[:, g * TPC:(g + 1) * TPC]).then_inc(stored, 16)
                sp.wait_ge(stored, GROUPS * 16)

            @block.tensor
            def _(pe):
                for t in range(T):
                    last = nc.tensor.transpose(mx_ps[t // 8][:, (t % 8) * P:(t % 8 + 1) * P], attn[:, t], id_f[:])
                    if t % TPC == TPC - 1:
                        last.then_inc(turned, 1)
                pe.wait_ge(later_in, 5 * 16)
                for g in range(GROUPS):
                    pe.wait_ge(turned_d if g % 2 else turned_a, g // 2 + 1)
                    for t in range(g * TPC, (g + 1) * TPC):
                        o = o_bank[g][:, (t % TPC) * P:(t % TPC + 1) * P]
                        nc.tensor.matmul(o, attn_t[:, t * P:(t + 1) * P], wo[:], start=True, stop=False)
                        last = nc.tensor.matmul(o, ones[:], bo_r[:], start=False, stop=True)
                    last.then_inc(projected, 1)
                for g in range(GROUPS):
                    pe.wait_ge(d_b, GROUPS + 2 * T + 2 + TPC * (g + 1))
                    for t in range(g * TPC, (g + 1) * TPC):
                        last = nc.tensor.transpose(mx_ps[t // 8][:, (t % 8) * P:(t % 8 + 1) * P], x1[:, t], id_f[:])
                    last.then_inc(x1_turned, 1)
                for g in range(GROUPS):
                    pe.wait_ge(x1_d if g % 2 else x1_a, g // 2 + 1)
                    for t in range(g * TPC, (g + 1) * TPC):
                        o = s_ps[0][:, t * NE:(t + 1) * NE]
                        nc.tensor.matmul(o, x1_t[:, t * P:(t + 1) * P], rw[:], start=True, stop=False)
                        last = nc.tensor.matmul(o, ones[:], rb_r[:], start=False, stop=True)
                last.then_inc(routed, 1)
                pe.wait_ge(d_b, D_WEIGHT)
                for g in range(GROUPS):
                    for t in range(g * TPC, (g + 1) * TPC):
                        last = nc.tensor.transpose(o_bank[g][0:NE, (t % TPC) * P:(t % TPC + 1) * P],
                                                   weight[:, t], id_f[:])
                    last.then_inc(w_turned, 1)
                pe.wait_ge(w_read, GROUPS)
                pe.sem_inc(silu_done, 2)
                pe.sem_inc(hid_done, 2)
                pe.sem_inc(hid_used, 2)
                pe.wait_ge(zeroed, 1)
                for c in range(NC):
                    nc.tensor.matmul(y_bank[c], zero_row[:, 0:P], zero_row[:], start=True, stop=True)

                def down(e, s, k):
                    c, f = divmod(k, FB)
                    pe.wait_ge(hid_done, e * UNITS + (k + 3))
                    nc.tensor.matmul(y_bank[c], wd[s][:, f, :], hid[:, k % 2], start=False, stop=True,
                                     skip_group_check=True).then_inc(hid_used, 1)

                with pe.Fori(0, TURNS) as i:
                    for s in range(2):
                        e = i * 2 + s
                        pe.wait_ge(wload[s], i * 64 + 64)
                        for k in range(UNITS):
                            c, f = divmod(k, FB)
                            sl = slice(c * BANK, (c + 1) * BANK)
                            pe.wait_ge(hid_done, e * UNITS + (k + 1))
                            if f == 0:
                                nc.tensor.matmul(pv_ps[k % 2][:], row_of[s][:], weight_t[:, sl],
                                                 start=True, stop=True).then_inc(w_full, 1)
                            pe.wait_ge(silu_done, e * UNITS + (k + 1))
                            nc.tensor.matmul(s_ps[k % 2][:], wg[s][:, f * P:(f + 1) * P], x1_t[:, sl],
                                             start=True, stop=True).then_inc(g_full, 1)
                            pe.wait_ge(xw_done, e * NC + (c + 1))
                            nc.tensor.matmul(pv_ps[k % 2][:], wu[s][:, f * P:(f + 1) * P], xw[:, sl],
                                             start=True, stop=True).then_inc(u_full, 1)
                            if k:
                                down(e, s, k - 1)
                        down(e, s, UNITS - 1)
                for g in range(GROUPS):
                    pe.wait_ge(y_kept, g + 1)
                    for t in range(g * TPC, (g + 1) * TPC):
                        last = nc.tensor.transpose(o_bank[g][:, (t % TPC) * P:(t % TPC + 1) * P],
                                                   moe_t[:, t * P:(t + 1) * P], id_f[:])
                    last.then_inc(y_turned, 1)

            @block.scalar
            def _(act):
                for g in range(0, GROUPS, 2):
                    act.wait_ge(turned, g + 1)
                    nc.scalar.activation(attn_t[:, g * BANK:(g + 1) * BANK], y_bank[g], ACT.Copy).then_inc(turned_a, 1)
                act.wait_ge(d_b, GROUPS + 2 * T + 1)
                nc.scalar.activation(std[:], std[:], ACT.Sqrt).then_inc(a_b, 1)
                for g in range(0, GROUPS, 2):
                    act.wait_ge(x1_turned, g + 1)
                    nc.scalar.activation(x1_t[:, g * BANK:(g + 1) * BANK], y_bank[g], ACT.Copy).then_inc(x1_a, 1)
                act.wait_ge(d_b, D_ROUTE + 2)
                nc.scalar.activation(e_gap[:], gap[:], ACT.Exp).then_inc(a_b, 1)
                for g in range(GROUPS):
                    act.wait_ge(w_turned, g + 1)
                    nc.scalar.activation(weight_t[:, g * BANK:(g + 1) * BANK], o_bank[g][0:NE, :],
                                         ACT.Copy).then_inc(w_read, 1)
                with act.Fori(0, TURNS) as i:
                    for s in range(2):
                        e = i * 2 + s
                        for k in range(UNITS):
                            act.wait_ge(g_full, e * UNITS + (k + 1))
                            act.wait_ge(hid_done, e * UNITS + (k + 1))
                            nc.scalar.activation(sg[:, k % 2], s_ps[k % 2][:], ACT.Silu).then_inc(silu_done, 1)
                act.wait_ge(hid_used, NE * UNITS + 2)
                for c in range(NC):
                    nc.scalar.activation(moe_t[:, c * BANK:(c + 1) * BANK], y_bank[c], ACT.Copy).then_inc(y_kept, 1)
                act.wait_ge(d_b, D_WEIGHT + GROUPS + 2 * T + 1)
                nc.scalar.activation(std[:], std[:], ACT.Sqrt).then_inc(a_b, 1)

            @block.vector
            def _(dve):
                nc.vector.memset(zero_row[:], 0.0).then_inc(zeroed, 1)
                for g in range(1, GROUPS, 2):
                    dve.wait_ge(turned, g + 1)
                    nc.vector.tensor_copy(attn_t[:, g * BANK:(g + 1) * BANK], y_bank[g]).then_inc(turned_d, 1)
                dve.wait_ge(x_here, 16)
                seq = link(dve, d_b, 0)
                for g in range(GROUPS):
                    dve.wait_ge(projected, g + 1)
                    sl = slice(g * TPC, (g + 1) * TPC)
                    nc.vector.tensor_tensor(y[:, sl], o_bank[g].rearrange("p (t c) -> p t c", c=C), x_in[:, sl],
                                            ALU.add).then_inc(d_b, 1)
                dve.wait_ge(d_b, GROUPS)
                k = norm(dve, seq, GROUPS, y, x1, 1)
                for g in range(1, GROUPS, 2):
                    dve.wait_ge(x1_turned, g + 1)
                    nc.vector.tensor_copy(x1_t[:, g * BANK:(g + 1) * BANK], y_bank[g]).then_inc(x1_d, 1)
                dve.wait_ge(routed, 1)
                seq(nc.vector.tensor_copy(logits.rearrange("p t e -> p (t e)"), s_ps[0][:, 0:T * NE]), k + 1)
                k += 1
                for t in range(T):
                    nc.vector.max(top[:, t], logits[:, t]).then_inc(d_b, 1)
                k += T
                dve.wait_ge(d_b, k)
                for t in range(T):
                    nc.vector.max_index(top_id[:, t], top[:, t], logits[:, t]).then_inc(d_b, 1)
                k += T
                dve.wait_ge(d_b, k)
                assert k == D_ROUTE
                seq(nc.vector.tensor_copy(top_f[:], top_id[:, :, 0:2]), k + 1)
                seq(nc.vector.tensor_tensor(gap[:], top[:, :, 1], top[:, :, 0], ALU.subtract), k + 2)
                dve.wait_ge(a_b, 2)
                seq(nc.vector.tensor_scalar(e_sum[:], e_gap[:], 1.0, None, ALU.add), k + 3)
                seq(nc.vector.reciprocal(gate[:, 0], e_sum[:]), k + 4)
                seq(nc.vector.tensor_tensor(gate[:, 1], e_gap[:], gate[:, 0], ALU.mult), k + 5)
                k += 5
                for j in range(2):
                    seq(nc.vector.tensor_tensor(pick[:, j], ids_sb[:].unsqueeze(1).to_broadcast([P, T, NE]),
                                                top_f[:, :, j:j + 1].to_broadcast([P, T, NE]), ALU.is_equal), k + 1)
                    seq(nc.vector.tensor_tensor(pick[:, j], pick[:, j],
                                                gate[:, j].unsqueeze(2).to_broadcast([P, T, NE]), ALU.mult), k + 2)
                    k += 2
                seq(nc.vector.tensor_tensor(weight[:], pick[:, 0], pick[:, 1], ALU.add), k + 1)
                k += 1
                assert k == D_WEIGHT
                with dve.Fori(0, TURNS) as i:
                    for s in range(2):
                        e = i * 2 + s
                        for kk in range(UNITS):
                            c, f = divmod(kk, FB)
                            if f == 0:
                                dve.wait_ge(w_full, e * NC + (c + 1))
                                nc.vector.tensor_tensor(xw[:, c * BANK:(c + 1) * BANK], pv_ps[kk % 2][:],
                                                        x1_t[:, c * BANK:(c + 1) * BANK],
                                                        ALU.mult).then_inc(xw_done, 1)
                            dve.wait_ge(silu_done, e * UNITS + (kk + 3))
                            dve.wait_ge(u_full, e * UNITS + (kk + 1))
                            dve.wait_ge(hid_used, e * UNITS + (kk + 1))
                            nc.vector.tensor_tensor(hid[:, kk % 2], sg[:, kk % 2], pv_ps[kk % 2][:],
                                                    ALU.mult).then_inc(hid_done, 1)
                for g in range(GROUPS):
                    dve.wait_ge(y_turned, g + 1)
                    sl = slice(g * TPC, (g + 1) * TPC)
                    nc.vector.tensor_tensor(y[:, sl], o_bank[g].rearrange("p (t c) -> p t c", c=C), x1[:, sl],
                                            ALU.add).then_inc(d_b, 1)
                k += GROUPS
                dve.wait_ge(d_b, k)
                norm(dve, seq, k, y, res, 3)


def constants():
    bf = mybir.dt.np(mybir.dt.bfloat16)
    freq = (1.0 / 10000.0 ** (np.arange(0, DK, 2, dtype=np.float32) / np.float32(DK))).astype(np.float32).astype(np.float64)
    pos = np.arange(S, dtype=np.float64)
    ang = freq[:, None] * pos[None, :]
    half = DK // 2
    sin8 = np.concatenate([np.sin(ang), np.sin(ang)])
    cos8 = np.concatenate([np.cos(ang), -np.cos(ang)])
    rot_sin = np.tile(sin8, (NH, 1)).astype(np.float32)
    rot_cos = np.tile(cos8, (NH, 1)).astype(np.float32)

    def parts(a):
        a = a.astype(np.float32)
        hi = a.astype(bf)
        r = a - hi.astype(np.float32)
        mid = r.astype(bf)
        return [hi, mid, (r - mid.astype(np.float32)).astype(bf)]

    def keys(shift):
        g = freq[:, None] * (pos - shift)[None, :]
        e = parts(np.concatenate([np.cos(g), np.sin(g)]))
        return np.concatenate([e[p] for p in K_PARTS])

    one = np.ones((3, S), bf)
    corner_q = np.zeros((CORNERS, S), bf)
    corner_k = np.zeros((CORNERS, S), bf)
    for t in range(CORNERS):
        corner_q[t, t * P + P - 1] = 1
        corner_k[t, (t + 1) * P] = NEG
    q, k = np.arange(P)[:, None], np.arange(P)[None, :]
    mask_low = np.where(k <= q, 0, NEG).astype(bf)
    fold = np.zeros((P, DK + 1), np.float32)
    for p in range(P):
        if p % 32 <= DK:
            fold[p, p % 32] = 1
    last = np.zeros((P, 1), np.float32)
    last[P - 1] = NEG
    rows = np.zeros((NE, NE, P), np.float32)
    for e in range(NE):
        rows[e, e] = 1
    return {
        "rot_sin": rot_sin, "rot_cos": rot_cos,
        "k_low_const": np.concatenate([keys(0), one]),
        "k_up_const": np.concatenate([keys(S), corner_k, one]),
        "q_up_const": corner_q,
        "mask_low4": np.tile(mask_low, (1, TPC)),
        "mask_up": np.where(k >= q + 2, 0, NEG).astype(bf),
        "ident_b": np.eye(P).astype(bf), "ident_f": np.eye(P, dtype=np.float32),
        "fold": fold, "last_token": last,
        "expert_ids": np.tile(np.arange(NE, dtype=np.float32), (P, 1)),
        "expert_rows": rows,
    }


def kernel(**inputs):
    import concourse.bacc as bacc
    from concourse.bass_utils import run_bass_kernel_spmd as run

    g = {k[3:]: np.asarray(v) for k, v in inputs.items()}
    wq, wk, wv = g["attn_Wq"], g["attn_Wk"], g["attn_Wv"]
    swap = lambda a: np.roll(a.reshape(a.shape[:-1] + (NH, DK)), DK // 2, axis=-1).reshape(a.shape)
    x = g["attn_x"][0]
    u, v = g["attn_u"].reshape(-1), g["attn_v"].reshape(-1)
    data = {
        "x_rows": x.reshape(T, P, C).transpose(1, 0, 2), "x_cols": x.T,
        "w_qkv": np.stack([wq, swap(wq), wk, wv], axis=1),
        "uv_cols": np.stack([u, v, swap(v)], axis=1), "u_row": u[None],
        "w_o": g["attn_Wo"], "bo_row": g["attn_bo"][None],
        "router_cols": g["ffn_router_w"].T, "router_bias": g["ffn_router_b"][None],
        "gate_cols": g["ffn_gate_w"].transpose(0, 2, 1), "up_cols": g["ffn_up_w"].transpose(0, 2, 1),
        "down_cols": g["ffn_down_w"].transpose(0, 2, 1).reshape(NE, FF // P, P, C).transpose(0, 2, 1, 3),
        **constants(),
    }
    nc = bacc.Bacc("TRN2", target_bir_lowering=False, num_devices=1)
    arrays, args = {}, {}
    for name, a in data.items():
        a = np.ascontiguousarray(a)
        arrays[name] = a
        args[name] = nc.dram_tensor(name, a.shape, mybir.dt.from_np(a.dtype), kind="ExternalInput").ap()
    for name in ("q_scratch", "r_scratch", "k_scratch"):
        args[name] = nc.dram_tensor(name, (NH, 3, DK, S), mybir.dt.bfloat16).ap()
    args["out"] = nc.dram_tensor("out", (1, S, C), mybir.dt.float32, kind="ExternalOutput").ap()
    build(nc, **args)
    r = run(nc, [arrays], core_ids=[0])
    return r.results[0]["out"]
```

```python
import concourse.bass as bass
from concourse import mybir
from concourse.alu_op_type import AluOpType as ALU
from contextlib import ExitStack
import numpy as np

S = 2048
C = 128
NH = 16
DK = C // NH
NE = 8
FF = 512
P = 128
T = S // P
BANK = 512
NC = S // BANK
TPC = BANK // P
NEG = -1.0e30
SCALE = float(DK) ** -0.5
EPS = 1e-5

Q_PARTS = [0, 1, 2, 0, 1, 0]
K_PARTS = [0, 0, 0, 1, 1, 2]
NP6 = len(Q_PARTS)
CONTENT = NP6 * DK
SCORE = 2 * CONTENT
CORNERS = T - 1
LOW_ROWS = SCORE + 3
UP_MAX_ROWS = SCORE + CORNERS
UP_ROWS = UP_MAX_ROWS + 3

TILES = NC * (T + 1)
PER_CHUNK = T + 1
PAIRS = 2 * T + 2
LEAD = 6
SBANKS = 3
LAG = 4
FIRST_LAG = 2
PSLOTS = PER_CHUNK
M_OPS = 8
F_OPS = 4
LOADS = 18
TOP = 2
BLOCKS = (TOP * S + NE * (P - 1)) // P
BLOCK_TURNS = (BLOCKS - 1) // 3
LOOP_FIRST, LOOP_TURNS = 1, 4


def head_items(h):
    items = []
    if h is None or h + 1 < NH:
        items += [("max", 1, j) for j in range(LEAD, PAIRS)]
    if h is None or h + 2 < NH:
        items += [("max", 2, j) for j in range(LEAD)]
    if h is None or h + 1 < NH:
        items.insert(PAIRS - LEAD + (2 if h is None or h + 2 < NH else 0), ("rows", 1, 0))
    if h is None or h > 0:
        items.insert(min(5, len(items)), ("result", -1, 0))
    return items


FIRST_ITEMS = [("max", 0, j) for j in range(PAIRS)] + [("rows", 0, 0)] + [("max", 1, j) for j in range(LEAD)]
LOOP_ITEMS = len(head_items(None))
RESULT_AT = head_items(None).index(("result", -1, 0))


def item_base(h):
    if isinstance(h, int):
        return len(FIRST_ITEMS) + sum(len(head_items(i)) for i in range(h))
    return (len(FIRST_ITEMS) + len(head_items(0)) - LOOP_ITEMS) + h * LOOP_ITEMS


class Head:

    def __init__(self, h, slot, nth, static):
        self.h, self.slot, self.nth, self.static = h, slot, nth, static

    def plus(self, n):
        s = self.slot + n
        return Head(self.h + n, s % 3, self.nth + s // 3, self.static)


def fixed(h):
    return Head(h, h % 3, h // 3, True)


def in_loop(i, s):
    return Head(i * 3 + s, s % 3, i + s // 3, False)


def build(nc, x_rows, x_cols, w_qkv, uv_cols, u_row, w_o, bo_row, router_cols, router_bias,
          gate_cols, up_cols, down_cols, rot_sin, rot_cos, k_low_const, k_up_const, q_up_const,
          mask_low4, mask_up, ident_b, ident_f, fold, last_token, expert_ids, steps, triangle, numbers, before,
          x_slots, y_slots, q_scratch, r_scratch, k_scratch, out):
    f32, bf16, u32 = mybir.dt.float32, mybir.dt.bfloat16, mybir.dt.uint32
    ACT, AX = mybir.ActivationFunctionType, mybir.AxisListType
    ctx = ExitStack()
    with ctx:
        def sb(name, shape, dt=f32):
            return ctx.enter_context(nc.sbuf_tensor(name, shape, dt))

        def ps(name, cols):
            return ctx.enter_context(nc.psum_tensor(name, [P, cols], f32))

        def sem(name):
            return ctx.enter_context(nc.semaphore(name))

        s_ps = [ps(f"s_ps{i}", BANK) for i in range(SBANKS)]
        mx_ps = [ps(f"mx_ps{i}", 2 * BANK) for i in range(2)]
        pv_ps = [ps("pv_ps", BANK), s_ps[2]]

        def link(eng, sem_, value):
            def f(ins, k):
                ins.then_inc(sem_, 1)
                eng.wait_ge(sem_, value + k)
            return f

        w_sb = sb("w_sb", [P, 4, C])
        uv = sb("uv", [P, 3])
        u_r = sb("u_r", [1, C])
        ones = sb("ones", [1, P])
        wo = sb("wo", [P, C])
        bo_r = sb("bo_r", [1, C])
        rw = sb("rw", [P, NE])
        rb_r = sb("rb_r", [1, NE])
        id_b = sb("id_b", [P, P], bf16)
        id_f = sb("id_f", [P, P])
        mk_low4 = sb("mk_low4", [P, BANK], bf16)
        mk_up = sb("mk_up", [P, P], bf16)
        fold_sb = sb("fold_sb", [P, DK + 1])
        last_sb = sb("last_sb", [P, 1])
        ids_sb = sb("ids_sb", [P, NE])
        steps_sb = sb("steps_sb", [P, T])
        tri_sb = sb("tri_sb", [P, NE * NE])
        numbers_sb = sb("numbers_sb", [1, BLOCKS])
        before_sb = sb("before_sb", [P, P], bf16)
        zeros = sb("zeros", [P, C])

        attn = sb("attn", [P, T, C])
        pro = ExitStack()

        def sa(name, shape, dt=f32):
            return pro.enter_context(nc.sbuf_tensor(name, shape, dt))

        q_low = [sa(f"q_low{i}", [LOW_ROWS, S], bf16) for i in range(3)]
        k_low = [sa(f"k_low{i}", [LOW_ROWS, S], bf16) for i in range(3)]
        q_up = [sa(f"q_up{i}", [UP_ROWS, S], bf16) for i in range(3)]
        k_up = [sa(f"k_up{i}", [UP_ROWS, S], bf16) for i in range(3)]
        v_head = [sa(f"v_head{i}", [P, T, 32]) for i in range(3)]
        probs = sa("probs", [P, PSLOTS, BANK])
        o_part = sa("o_part", [P, S])
        proj = sa("proj", [P, T, 4, C])
        s_next = sa("s_next", [P, NH, T])
        red = sa("red", [P, 3, T, 2])
        red_d = sa("red_d", [P, 3, T])
        m_a = sa("m_a", [P, 3, T])
        m_b = sa("m_b", [P, 3, T])
        m_max = sa("m_max", [P, 3, T])
        m_rest = sa("m_rest", [P, 3, T])
        m_parts = sa("m_parts", [P, 3, 3, T], bf16)
        m_rows = sa("m_rows", [3 * T, 3, P], bf16)
        d_next = sa("d_next", [P, 3, T])
        p_next = sa("p_next", [P, 3, T])
        f_next = sa("f_next", [P, T, DK])
        f_den = sa("f_den", [P, T])
        f_rden = sa("f_rden", [P, T])
        f_num = sa("f_num", [P, T, DK])
        tiles_seen = sem("tiles_seen")
        s_full, s_read = sem("s_full"), sem("s_read")
        p_free, picked = sem("p_free"), sem("picked")
        mx_full, mx_read = sem("mx_full"), sem("mx_read")
        o_read = sem("o_read")
        v_ready, next_ready = sem("v_ready"), sem("next_ready")
        m_chain, f_chain = sem("m_chain"), sem("f_chain")
        stacked = [sem(f"stacked{i}") for i in range(3)]
        m_placed = [sem(f"m_placed{i}") for i in range(3)]
        consts = sem("consts")
        w_in, tab_in, later_in = sem("w_in"), sem("tab_in"), sem("later_in")
        pads, filled, slots_clear = sem("pads"), sem("filled"), sem("slots_clear")
        q_full, k_full, row_full = sem("q_full"), sem("k_full"), sem("row_full")
        a_proj, a_hi, a_row = sem("a_proj"), sem("a_hi"), sem("a_row")
        g_rot, g_prod = sem("g_rot"), sem("g_prod")
        d_pro = sem("d_pro")
        kept = sem("kept")

        with pro, nc.Block() as block:
            def tmp(name, shape, dt=f32):
                return pro.enter_context(nc.sbuf_tensor(name, shape, dt))

            xt = tmp("xt", [P, S + 1])
            t_sin = tmp("t_sin", [P, S])
            t_cos = tmp("t_cos", [P, S])
            qu, qv, qs, kf = (probs[:, i * NC:(i + 1) * NC].rearrange("p c n -> p (c n)") for i in range(4))
            split = [tmp(f"split{i}", [P, 3, 2 * BANK], bf16) for i in range(3)]


            def max_tile(pe, hd, j, bank):
                s = hd.slot
                if j >= 2 * T:
                    for b in range(2):
                        nc.tensor.matmul(bank[:, b * BANK:(b + 1) * BANK], id_b[:], mk_low4[:],
                                         start=True, stop=True)
                        for i in range(TPC):
                            t = 8 * (j - 2 * T) + TPC * b + i
                            c0 = b * BANK + i * P
                            last = nc.tensor.matmul(bank[:, c0:c0 + P], q_low[s][0:SCORE, t * P:(t + 1) * P],
                                                    k_low[s][0:SCORE, t * P:(t + 1) * P],
                                                    start=False, stop=True, skip_group_check=True)
                    return last
                t, half = j // 2, j % 2
                for b in range(2):
                    kc = 2 * half + b
                    left = min(max(t - TPC * kc, 0), TPC) * P
                    o = b * BANK
                    k0 = kc * BANK
                    if left:
                        last = nc.tensor.matmul(bank[:, o:o + left], q_low[s][0:SCORE, t * P:(t + 1) * P],
                                                k_low[s][0:SCORE, k0:k0 + left], start=True, stop=True)
                    if left < BANK:
                        last = nc.tensor.matmul(bank[:, o + left:o + BANK],
                                                q_up[s][0:UP_MAX_ROWS, t * P:(t + 1) * P],
                                                k_up[s][0:UP_MAX_ROWS, k0 + left:k0 + BANK],
                                                start=True, stop=True)
                        if t // TPC == kc:
                            last = nc.tensor.matmul(bank[:, o + left:o + left + P], id_b[:], mk_up[:],
                                                    start=False, stop=True, skip_group_check=True)
                return last

            def pe_item(pe, hd, item, number, slot):
                kind, ahead, j = item
                of = hd.plus(ahead)
                bank = mx_ps[slot]
                if kind == "max" and j == 0:
                    pe.wait_ge(stacked[of.slot], (of.nth + 1) * (16 * LOADS))
                if kind == "rows":
                    pe.wait_ge(m_chain, (of.h + 1) * M_OPS)
                if kind == "result":
                    pe.wait_ge(o_read, (of.h + 1) * NC + 1)
                pe.wait_ge(mx_read, number + 1)
                if kind == "max":
                    last = max_tile(pe, of, j, bank)
                elif kind == "rows":
                    last = nc.tensor.matmul(bank[0:3 * T, 0:P],
                                            m_parts[:, of.slot].rearrange("p a t -> p (a t)"), id_b[:],
                                            start=True, stop=True)
                else:
                    for t in range(T):
                        last = nc.tensor.matmul(bank[:, t * (DK + 1):(t + 1) * (DK + 1)],
                                                o_part[:, t * P:(t + 1) * P], fold_sb[:],
                                                start=True, stop=True)
                last.then_inc(mx_full, 1)

            def score_bank(hd, n):
                return s_ps[(hd.slot * TILES + n) % SBANKS]

            def pe_scores(pe, hd, n):
                s, (c, kb) = hd.slot, divmod(n, PER_CHUNK)
                if n == 0:
                    pe.wait_ge(m_placed[s], (hd.nth + 1) * 32)
                pe.wait_ge(s_read, hd.h * TILES + (n + NC - SBANKS + 1))
                bank = score_bank(hd, n)
                q0 = c * BANK
                if kb == T:
                    for i in range(TPC):
                        t = TPC * c + i
                        last = nc.tensor.matmul(bank[:, i * P:(i + 1) * P], k_low[s][0:LOW_ROWS, t * P:(t + 1) * P],
                                                q_low[s][0:LOW_ROWS, t * P:(t + 1) * P],
                                                start=True, stop=True)
                else:
                    up = min(max(kb - TPC * c + 1, 0), TPC) * P
                    if up:
                        last = nc.tensor.matmul(bank[:, 0:up], k_up[s][0:UP_ROWS, kb * P:(kb + 1) * P],
                                                q_up[s][0:UP_ROWS, q0:q0 + up], start=True, stop=True)
                    if up < BANK:
                        last = nc.tensor.matmul(bank[:, up:BANK], k_low[s][0:LOW_ROWS, kb * P:(kb + 1) * P],
                                                q_low[s][0:LOW_ROWS, q0 + up:q0 + BANK], start=True, stop=True)
                last.then_inc(s_full, 1)

            def pe_values(pe, hd, n):
                s, (c, kb) = hd.slot, divmod(n, PER_CHUNK)
                if n == 0:
                    pe.wait_ge(v_ready, hd.h + 1)
                if kb == 0:
                    pe.wait_ge(o_read, hd.h * NC + (c + 1))
                on_diagonal = kb == T or kb // TPC == c
                if on_diagonal:
                    i = TPC if kb == T else kb - TPC * c
                    pe.wait_ge(picked, hd.h * (NC * (TPC + 1)) + (c * (TPC + 1) + i + 1))
                else:
                    pe.wait_ge(s_read, hd.h * TILES + (n + NC + 1))
                bank, src = pv_ps[0], probs[:, n % PER_CHUNK]
                if kb == T:
                    for i in range(TPC):
                        last = nc.tensor.matmul(bank[32 * i:32 * i + 32, i * P:(i + 1) * P],
                                                v_head[s][:, TPC * c + i, :], src[:, i * P:(i + 1) * P],
                                                start=False, stop=True, skip_group_check=True)
                else:
                    g = kb % 4
                    last = nc.tensor.matmul(bank[32 * g:32 * g + 32, :], v_head[s][:, kb, :], src,
                                            start=(kb < 4), stop=True, skip_group_check=True)
                last.then_inc(p_free, 1)

            def pe_head(pe, hd):
                items = head_items(hd.h if hd.static else None)
                base = item_base(hd.h)
                even = (item_base(hd.h) if hd.static else item_base(LOOP_FIRST)) % 2
                at = 0
                for n in range(TILES + LAG):
                    if n < TILES:
                        while at < len(items) and at * TILES < (n + 1) * len(items) and (
                                items[at][0] != "result" or n >= 2 * LAG + 2):
                            pe_item(pe, hd, items[at], base + at, (even + at) % 2)
                            at += 1
                        pe_scores(pe, hd, n)
                    if n >= LAG and (n - LAG) % PER_CHUNK == T:
                        for m in range(n - LAG - 4, n - LAG + 1):
                            pe_values(pe, hd, m)
                    elif n >= LAG + FIRST_LAG and (n - LAG - FIRST_LAG) % PER_CHUNK == 3:
                        for m in range(n - LAG - FIRST_LAG - 3, n - LAG - FIRST_LAG + 1):
                            pe_values(pe, hd, m)
                    elif n >= LAG and (n - LAG) % PER_CHUNK in (7, 11):
                        for m in range(n - LAG - 3, n - LAG + 1):
                            pe_values(pe, hd, m)

            def dve_maximum(dve, of):
                s = of.slot
                seq = link(dve, m_chain, of.h * M_OPS)
                seq(nc.vector.tensor_tensor(m_a[:, s], red[:, s, :, 0], red[:, s, :, 1], ALU.max), 1)
                seq(nc.vector.tensor_tensor(m_b[:, s], m_a[:, s], red_d[:, s], ALU.max), 2)
                seq(nc.vector.tensor_tensor(m_max[:, s], m_b[:, s], s_next[:, of.h, :], ALU.max), 3)
                seq(nc.vector.tensor_scalar(m_parts[:, s, 0], m_max[:, s], -1.0, None, ALU.mult), 4)
                seq(nc.vector.scalar_tensor_tensor(out=m_rest[:, s], in0=m_max[:, s], scalar=-1.0,
                                                   in1=m_parts[:, s, 0], op0=ALU.mult, op1=ALU.subtract), 5)
                seq(nc.vector.tensor_copy(m_parts[:, s, 1], m_rest[:, s]), 6)
                seq(nc.vector.tensor_tensor(m_parts[:, s, 2], m_rest[:, s], m_parts[:, s, 1], ALU.subtract), 7)
                nc.vector.tensor_tensor(d_next[:, s], s_next[:, of.h, :], m_max[:, s],
                                        ALU.subtract).then_inc(m_chain, 1)

            def dve_item(dve, hd, item, number, slot):
                kind, ahead, j = item
                of = hd.plus(ahead)
                bank, s = mx_ps[slot], of.slot
                dve.wait_ge(mx_full, number + 1)
                if kind == "max" and j < 2 * T:
                    nc.vector.reduce_max(red[:, s, j // 2, j % 2:j % 2 + 1], bank[:, :],
                                         AX.X).then_inc(mx_read, 1)
                elif kind == "max":
                    t0 = 8 * (j - 2 * T)
                    nc.vector.reduce_max(red_d[:, s, t0:t0 + 8], bank.rearrange("p (t k) -> p t k", k=P),
                                         AX.X).then_inc(mx_read, 1)
                    if j == PAIRS - 1:
                        dve.wait_ge(mx_read, number + 3)
                        dve_maximum(dve, of)
                elif kind == "rows":
                    nc.vector.tensor_copy(m_rows[:, s], bank[0:3 * T, 0:P]).then_inc(mx_read, 1)
                else:
                    seq = link(dve, f_chain, of.h * F_OPS)
                    dve.wait_ge(next_ready, of.h + 1)
                    o = bank[:, 0:T * (DK + 1)].rearrange("p (t d) -> p t d", d=DK + 1)
                    pn = p_next[:, s]
                    seq(nc.vector.tensor_tensor(f_next[:], proj[:, :, 3, bass.ds(of.h * DK, DK)],
                                                pn.unsqueeze(2).to_broadcast([P, T, DK]), ALU.mult), 1)
                    seq(nc.vector.tensor_tensor(f_den[:], o[:, :, DK], pn, ALU.add), 2)
                    seq(nc.vector.reciprocal(f_rden[:], f_den[:]), 3)
                    ins = nc.vector.tensor_tensor(f_num[:], o[:, :, 0:DK], f_next[:], ALU.add)
                    ins.then_inc(mx_read, 1)
                    dve.wait_ge(mx_read, number + 3)
                    seq(nc.vector.tensor_tensor(attn[:, :, bass.ds(of.h * DK, DK)], f_num[:],
                                                f_rden[:].unsqueeze(2).to_broadcast([P, T, DK]), ALU.mult), 4)

            def dve_head(dve, hd):
                base = item_base(hd.h)
                even = (item_base(hd.h) if hd.static else item_base(LOOP_FIRST)) % 2
                for i, item in enumerate(head_items(hd.h if hd.static else None)):
                    dve_item(dve, hd, item, base + i, (even + i) % 2)

            def act_result(act, hd, c):
                act.wait_ge(p_free, hd.h * TILES + ((c + 1) * PER_CHUNK + PSLOTS))
                nc.scalar.activation(o_part[:, c * BANK:(c + 1) * BANK], pv_ps[0][:],
                                     ACT.Copy).then_inc(o_read, 1)

            def act_next(act, of):
                act.wait_ge(m_chain, (of.h + 1) * M_OPS)
                nc.scalar.activation(p_next[:, of.slot], d_next[:, of.slot], ACT.Exp,
                                     scale=SCALE).then_inc(next_ready, 1)

            def act_head(act, hd):
                for n in range(TILES):
                    act.wait_ge(s_full, hd.h * TILES + (n + 1))
                    act.wait_ge(p_free, hd.h * TILES + (n + 1))
                    nc.scalar.activation(probs[:, n % PER_CHUNK], score_bank(hd, n)[:], ACT.Exp,
                                         scale=SCALE).then_inc(s_read, 1)
                    c, i = divmod(n, PER_CHUNK)
                    if i == LAG + 2:
                        if c:
                            if c == 1 and not (hd.static and hd.h == 0):
                                act.wait_ge(mx_full, item_base(hd.h) + (RESULT_AT + 1 if not hd.static else
                                            head_items(hd.h).index(("result", -1, 0)) + 1))
                            act_result(act, hd, c - 1)
                        elif not (hd.static and hd.h == 0):
                            act_result(act, hd.plus(-1) if hd.static else Head(hd.h - 1, 0, 0, False), NC - 1)
                    if n == TILES - 2 and not (hd.static and hd.h + 1 >= NH):
                        act_next(act, hd.plus(1))

            def pool_values(pool, of):
                nc.gpsimd.tensor_copy(v_head[of.slot][:, :, 0:DK],
                                      proj[:, :, 1, bass.ds(of.h * DK, DK)]).then_inc(v_ready, 1)

            def pool_head(pool, hd):
                for c in range(NC):
                    for i in range(TPC + 1):
                        n = c * PER_CHUNK + (TPC * c + i if i < TPC else T)
                        pool.wait_ge(s_read, hd.h * TILES + (n + NC + 1))
                        pool.sem_inc(tiles_seen, 1)
                        if i < TPC:
                            v = probs[:, n % PER_CHUNK, i * P:(i + 1) * P]
                            nc.gpsimd.affine_select(out=v, in_=v, compare_op=ALU.is_ge, fill=0.0, base=-2,
                                                    pattern=[[-1, P]], channel_multiplier=1).then_inc(picked, 1)
                        else:
                            v = probs[:, n % PER_CHUNK, :].rearrange("p (t q) -> p t q", q=P)
                            nc.gpsimd.affine_select(out=v, in_=v, compare_op=ALU.is_ge, fill=0.0, base=0,
                                                    pattern=[[0, TPC], [1, P]],
                                                    channel_multiplier=-1).then_inc(picked, 1)
                        if c == 0 and i == 0 and not (hd.static and hd.h + 1 >= NH):
                            pool_values(pool, hd.plus(1))

            def stack(sp, of):
                s = of.slot

                def put(dst, row0, parts, src):
                    n = len(parts)
                    step = parts[1] - parts[0] if n > 1 else 1
                    a = src[of.h, parts[0]:parts[0] + 1]
                    if step == 0:
                        a = a.to_broadcast([n, DK, a.shape[2]])
                    else:
                        a = src[of.h, parts[0]:parts[0] + n]
                    sp.dma_start(dst[row0:row0 + n * DK, 0:a.shape[2]], a).then_inc(stacked[s], 16)

                for row, lo, n in ((0, 0, 3), (3, 3, 2), (5, 5, 1)):
                    qp, kp = Q_PARTS[lo:lo + n], K_PARTS[lo:lo + n]
                    put(k_low[s], row * DK, kp, k_scratch)
                    put(k_up[s], row * DK, kp, k_scratch)
                    put(q_low[s], row * DK, qp, q_scratch)
                    put(q_up[s], row * DK, qp, q_scratch)
                    put(q_low[s], CONTENT + row * DK, qp, r_scratch)
                    put(q_up[s], CONTENT + row * DK, qp, r_scratch[:, :, :, 1:S])

            def place_maximum(sp, of):
                s = of.slot
                sp.wait_ge(mx_read, item_of_rows(of) + 3)
                for dst, r0 in ((q_low[s], SCORE), (q_up[s], UP_MAX_ROWS)):
                    sp.dma_start(dst[r0:r0 + 3, :], m_rows[:, s]).then_inc(m_placed[s], 16)

            def item_of_rows(of):
                if of.static:
                    if of.h == 0:
                        return PAIRS
                    return item_base(of.h - 1) + head_items(of.h - 1).index(("rows", 1, 0))
                return item_base(of.h - 1) + head_items(None).index(("rows", 1, 0))

            def sp_head(sp, hd):
                if not (hd.static and hd.h + 2 >= NH):
                    if not (hd.static and hd.h == 0):
                        sp.wait_ge(s_full, hd.h * TILES)
                    stack(sp, hd.plus(2))
                if not (hd.static and hd.h + 1 >= NH):
                    place_maximum(sp, hd.plus(1))

            def all_heads(eng, step):
                for h in range(LOOP_FIRST):
                    step(eng, fixed(h))
                with eng.Fori(0, LOOP_TURNS) as i:
                    for s in range(LOOP_FIRST, LOOP_FIRST + 3):
                        step(eng, in_loop(i, s))
                for h in range(LOOP_FIRST + 3 * LOOP_TURNS, NH):
                    step(eng, fixed(h))


            def split_done(half, i):
                return (2 * half + 1) * 11 + 2 + 3 * (i + 1)

            @block.sync
            def _(sp):
                sp.dma_start(w_sb[:], w_qkv).then_inc(w_in, 16)
                sp.dma_start(uv[:], uv_cols).then_inc(w_in, 16)
                sp.dma_start(u_r[:], u_row).then_inc(w_in, 16)
                for c in range(NC):
                    sp.dma_start(xt[:, c * BANK:(c + 1) * BANK], x_cols[:, c * BANK:(c + 1) * BANK]).then_inc(w_in, 16)
                sp.dma_start(t_sin[:], rot_sin).then_inc(tab_in, 16)
                sp.dma_start(t_cos[:], rot_cos).then_inc(tab_in, 16)
                for dst, src in ((id_b, ident_b), (id_f, ident_f), (mk_low4, mask_low4), (mk_up, mask_up),
                                 (fold_sb, fold), (last_sb, last_token)):
                    sp.dma_start(dst[:], src).then_inc(consts, 16)
                for i in range(3):
                    sp.dma_start(k_low[i][CONTENT:LOW_ROWS, :], k_low_const).then_inc(consts, 16)
                    sp.dma_start(k_up[i][CONTENT:UP_ROWS, :], k_up_const).then_inc(consts, 16)
                    sp.dma_start(q_up[i][SCORE:UP_MAX_ROWS, :], q_up_const).then_inc(consts, 16)
                for dst, src in ((wo, w_o), (bo_r, bo_row), (rw, router_cols), (rb_r, router_bias),
                                 (ids_sb, expert_ids), (steps_sb, steps), (tri_sb, triangle),
                                 (numbers_sb, numbers), (before_sb, before)):
                    sp.dma_start(dst[:], src).then_inc(later_in, 16)
                for half in range(2):
                    for i, dst in enumerate((q_scratch, r_scratch, k_scratch)):
                        sp.wait_ge(d_pro, split_done(half, i))
                        for part in range(3):
                            sp.dma_start(dst[:, part, :, half * 2 * BANK:(half + 1) * 2 * BANK],
                                         split[i][:, part]).then_inc(kept, 16)
                sp.wait_ge(kept, 18 * 16)
                sp.wait_ge(filled, 9)
                stack(sp, fixed(0))
                stack(sp, fixed(1))
                place_maximum(sp, fixed(0))
                sp.wait_ge(pads, 3)
                for b in range(BLOCKS):
                    sp.dma_start(x_slots[b * P:(b + 1) * P, :], zeros[:]).then_inc(slots_clear, 16)
                all_heads(sp, sp_head)

            @block.tensor
            def _(pe):
                pe.sem_inc(p_free, PSLOTS)
                pe.sem_inc(mx_read, 2)
                pe.sem_inc(o_read, 1)
                pe.wait_ge(w_in, 7 * 16)
                pe.wait_ge(pads, 3)
                for c in range(NC):
                    cols = xt[:, c * BANK:(c + 1) * BANK]
                    if c >= 2:
                        pe.wait_ge(a_proj, 4 * (c - 1))
                    nc.tensor.matmul(mx_ps[c % 2][:, 0:BANK], w_sb[:, 0, :], cols, start=True, stop=True)
                    nc.tensor.matmul(mx_ps[c % 2][:, BANK:], w_sb[:, 1, :], cols,
                                     start=True, stop=True).then_inc(q_full, 1)
                    nc.tensor.matmul(s_ps[c % 2][:], w_sb[:, 2, :], cols, start=True, stop=True).then_inc(k_full, 1)
                    for t in range(TPC * c, TPC * (c + 1)):
                        if t >= 2:
                            pe.wait_ge(a_row, t - 1)
                        bank, here = pv_ps[t % 2], xt[:, t * P:(t + 1) * P]
                        nc.tensor.matmul(bank[:, 0:P], here, w_sb[:, 0, :], start=True, stop=False)
                        nc.tensor.matmul(bank[:, 0:P], ones[:], u_r[:], start=False, stop=True)
                        nc.tensor.matmul(bank[:, P:2 * P], here, w_sb[:, 3, :], start=True, stop=True)
                        nc.tensor.matmul(bank[:, 2 * P:], xt[:, t * P + 1:(t + 1) * P + 1],
                                         w_sb[:, 2:4, :].rearrange("p a c -> p (a c)"),
                                         start=True, stop=True).then_inc(row_full, 1)
                pe.wait_ge(consts, 15 * 16)
                pe.wait_ge(filled, 9)
                pe.wait_ge(a_proj, 4 * NC)
                pe.wait_ge(a_row, T)
                for i, item in enumerate(FIRST_ITEMS):
                    pe_item(pe, fixed(0), item, i, i % 2)
                all_heads(pe, pe_head)
                pe_item(pe, fixed(NH), ("result", -1, 0), item_base(NH), item_base(NH) % 2)

            @block.scalar
            def _(act):
                act.wait_ge(w_in, 7 * 16)
                for c in range(NC):
                    sl = slice(c * BANK, (c + 1) * BANK)
                    act.wait_ge(q_full, c + 1)
                    nc.scalar.activation(qv[:, sl], mx_ps[c % 2][:, 0:BANK], ACT.Identity,
                                         bias=uv[:, 1:2]).then_inc(a_proj, 1)
                    nc.scalar.activation(qs[:, sl], mx_ps[c % 2][:, BANK:], ACT.Identity,
                                         bias=uv[:, 2:3]).then_inc(a_proj, 1)
                    nc.scalar.activation(qu[:, sl], mx_ps[c % 2][:, 0:BANK], ACT.Identity,
                                         bias=uv[:, 0:1]).then_inc(a_proj, 1)
                    act.wait_ge(k_full, c + 1)
                    nc.scalar.activation(kf[:, sl], s_ps[c % 2][:], ACT.Copy).then_inc(a_proj, 1)
                    act.wait_ge(a_proj, 4 * (c + 1))
                    if c >= 2:
                        act.wait_ge(kept, 9 * 16)
                    o = (c % 2) * BANK
                    nc.scalar.activation(split[0][:, 0, o:o + BANK], qu[:, sl], ACT.Copy).then_inc(a_hi, 1)
                    nc.scalar.activation(split[2][:, 0, o:o + BANK], kf[:, sl], ACT.Copy).then_inc(a_hi, 1)
                    act.wait_ge(d_pro, c * 11 + 2)
                    nc.scalar.activation(split[1][:, 0, o:o + BANK], qv[:, sl], ACT.Copy).then_inc(a_hi, 1)
                    for t in range(TPC * c, TPC * (c + 1)):
                        act.wait_ge(row_full, t + 1)
                        nc.scalar.activation(proj[:, t].rearrange("p a c -> p (a c)"), pv_ps[t % 2][:],
                                             ACT.Copy).then_inc(a_row, 1)
                act.sem_inc(s_read, NC)
                act_next(act, fixed(0))
                all_heads(act, act_head)
                act_result(act, fixed(NH - 1), NC - 1)

            @block.vector
            def _(dve):
                nc.vector.memset(xt[:, S:S + 1], 0.0).then_inc(pads, 1)
                nc.vector.memset(ones[:], 1.0).then_inc(pads, 1)
                nc.vector.memset(zeros[:], 0.0).then_inc(pads, 1)
                dve.wait_ge(tab_in, 32)
                seq = link(dve, d_pro, 0)
                k = 0
                for c in range(NC):
                    sl = slice(c * BANK, (c + 1) * BANK)
                    o = (c % 2) * BANK
                    dve.wait_ge(a_proj, 4 * c + 3)
                    seq(nc.vector.tensor_tensor(qv[:, sl], qv[:, sl], t_sin[:, sl], ALU.mult), k + 1)
                    dve.wait_ge(g_rot, c + 1)
                    seq(nc.vector.tensor_tensor(qv[:, sl], qv[:, sl], qs[:, sl], ALU.add), k + 2)
                    k += 2
                    for i, src in ((0, qu), (1, qv), (2, kf)):
                        dve.wait_ge(a_hi, 3 * (c + 1))
                        seq(nc.vector.tensor_tensor(src[:, sl], src[:, sl], split[i][:, 0, o:o + BANK], ALU.subtract), k + 1)
                        seq(nc.vector.tensor_copy(split[i][:, 1, o:o + BANK], src[:, sl]), k + 2)
                        seq(nc.vector.tensor_tensor(split[i][:, 2, o:o + BANK], src[:, sl],
                                                    split[i][:, 1, o:o + BANK], ALU.subtract), k + 3)
                        k += 3
                dve.wait_ge(g_prod, 1)
                seq(nc.vector.reduce_sum(s_next.rearrange("p h t -> p t h"),
                                         proj[:, :, 0, :].rearrange("p t (h d) -> p t h d", d=DK), AX.X), k + 1)
                seq(nc.vector.tensor_scalar(s_next[:, :, T - 1], s_next[:, :, T - 1], last_sb[:], None, ALU.add), k + 2)
                for i, item in enumerate(FIRST_ITEMS):
                    dve_item(dve, fixed(0), item, i, i % 2)
                all_heads(dve, dve_head)
                dve_item(dve, fixed(NH), ("result", -1, 0), item_base(NH), item_base(NH) % 2)

            @block.gpsimd
            def _(pool):
                for i in range(3):
                    nc.gpsimd.memset(v_head[i][:, :, DK:DK + 1], 1.0).then_inc(filled, 1)
                    nc.gpsimd.memset(v_head[i][:, :, DK + 1:], 0.0).then_inc(filled, 1)
                    nc.gpsimd.memset(q_up[i][0:SCORE, S - 1:S], 0.0).then_inc(filled, 1)
                pool.wait_ge(tab_in, 32)
                for c in range(NC):
                    sl = slice(c * BANK, (c + 1) * BANK)
                    pool.wait_ge(a_proj, 4 * c + 2)
                    nc.gpsimd.tensor_tensor(qs[:, sl], qs[:, sl], t_cos[:, sl], ALU.mult).then_inc(g_rot, 1)
                pool.wait_ge(a_row, T)
                nc.gpsimd.tensor_tensor(proj[:, :, 0, :], proj[:, :, 0, :], proj[:, :, 2, :],
                                        ALU.mult).then_inc(g_prod, 1)
                pool_values(pool, fixed(0))
                all_heads(pool, pool_head)

        with ExitStack() as late, nc.Block() as block:
            def tmp(name, shape, dt=f32):
                return late.enter_context(nc.sbuf_tensor(name, shape, dt))

            def sem_b(name):
                return late.enter_context(nc.semaphore(name))

            GROUPS = NC
            FB = FF // P
            x_in = tmp("x_in", [P, T, C])
            attn_t = tmp("attn_t", [P, S])
            y = tmp("y", [P, T, C])
            x1 = tmp("x1", [P, T, C])
            x1_t = tmp("x1_t", [P, S])
            stats = tmp("stats", [P, T, 6])
            mean_var = tmp("mean_var", [P, T, 2])
            std = tmp("std", [P, T])
            rstd = tmp("rstd", [P, T])
            logits = tmp("logits", [P, T, NE])
            top = tmp("top", [P, T, 8])
            top_id = tmp("top_id", [P, T, 8], u32)
            top_f = tmp("top_f", [P, T, 2])
            gap = tmp("gap", [P, T])
            e_gap = tmp("e_gap", [P, T])
            e_sum = tmp("e_sum", [P, T])
            gate = tmp("gate", [P, 2, T])
            pick = tmp("pick", [P, 2, T, NE])
            picks = tmp("picks", [P, T, NE])
            picks_b = tmp("picks_b", [P, T, NE], bf16)
            ones_b = tmp("ones_b", [P, P], bf16)
            count = tmp("count", [P, NE])
            over = tmp("over", [P, NE, T])
            n_blocks = tmp("n_blocks", [P, NE])
            over8 = tmp("over8", [P, NE, NE])
            start = tmp("start", [P, NE])
            stop_at = tmp("stop_at", [P, NE])
            start128 = tmp("start128", [P, NE])
            slot_of = tmp("slot_of", [P, T, NE])
            slot_j = tmp("slot_j", [P, TOP, T, NE])
            slot_f = tmp("slot_f", [P, TOP, T])
            slot_u = tmp("slot_u", [P, TOP, T], u32)
            past = tmp("past", [1, BLOCKS, NE])
            owner_f = tmp("owner_f", [1, BLOCKS])
            owner_g = tmp("owner_g", [1, BLOCKS])
            owner = tmp("owner", [1, BLOCKS], mybir.dt.int32)
            wg = tmp("wg", [P, NE * FF])
            wu = tmp("wu", [P, NE * FF])
            wd = tmp("wd", [P, NE * FF])
            x_blk = tmp("x_blk", [P, 3, C])
            x_blk_t = tmp("x_blk_t", [P, 3, P])
            sg = tmp("sg", [P, 3, FF])
            hid = tmp("hid", [P, 3, FF])
            hid_t = tmp("hid_t", [P, 3, FF])
            y_blk = tmp("y_blk", [P, 3, C])
            back = tmp("back", [P, TOP, T, C])
            res = tmp("res", [P, T, C])

            x_here, wload, turned = sem_b("x_here"), sem_b("wload"), sem_b("turned")
            turned_a, turned_d = sem_b("turned_a"), sem_b("turned_d")
            projected, d_b, a_b = sem_b("projected"), sem_b("d_b"), sem_b("a_b")
            routed = sem_b("routed")
            x1_turned, x1_a, x1_d = sem_b("x1_turned"), sem_b("x1_a"), sem_b("x1_d")
            ones_set, ranked, scattered = sem_b("ones_set"), sem_b("ranked"), sem_b("scattered")
            x_got = [sem_b(f"x_got{i}") for i in range(3)]
            y_put = [sem_b(f"y_put{i}") for i in range(3)]
            x_turned, x_kept = sem_b("x_turned"), sem_b("x_kept")
            g_full, silu_done, u_full = sem_b("g_full"), sem_b("silu_done"), sem_b("u_full")
            hid_done, t_full, t_kept = sem_b("hid_done"), sem_b("t_full"), sem_b("t_kept")
            y_full, y_kept, stored = sem_b("y_full"), sem_b("y_kept"), sem_b("stored")
            gathered = [sem_b(f"gathered{g}") for g in range(GROUPS)]
            o_bank = [s_ps[0], s_ps[1], pv_ps[0], pv_ps[1]]
            half_bank = [mx_ps[c // 2][:, (c % 2) * BANK:(c % 2 + 1) * BANK] for c in range(NC)]
            g_ps, u_ps, t_ps = s_ps[0], s_ps[1], pv_ps[0]
            xt_ps, y_ps = mx_ps[0][:, 0:P], mx_ps[1][:, 0:C]

            def block_steps(eng, step):
                step(eng, 0, 0, 0)
                with eng.Fori(0, BLOCK_TURNS) as i:
                    for s in range(1, 4):
                        step(eng, i * 3 + s, s % 3, i + s // 3)
                for b in range(1 + 3 * BLOCK_TURNS, BLOCKS):
                    step(eng, b, b % 3, b // 3)

            def is_last(b):
                return isinstance(b, int) and b == BLOCKS - 1

            def is_first(b):
                return isinstance(b, int) and b == 0

            def norm(dve, seq, k, src, dst, wait_sqrt, t0=0, t1=T):
                for t in range(t0, t1):
                    nc.vector.bn_stats(stats[:, t], src[:, t]).then_inc(d_b, 1)
                k += t1 - t0
                dve.wait_ge(d_b, k)
                for t in range(t0, t1):
                    nc.vector.bn_aggr(mean_var[:, t], stats[:, t]).then_inc(d_b, 1)
                k += t1 - t0
                dve.wait_ge(d_b, k)
                seq(nc.vector.tensor_scalar(std[:, t0:t1], mean_var[:, t0:t1, 1], EPS, None, ALU.add), k + 1)
                dve.wait_ge(a_b, wait_sqrt)
                seq(nc.vector.reciprocal(rstd[:, t0:t1], std[:, t0:t1]), k + 2)
                k += 2
                for t in range(t0, t1):
                    nc.vector.tensor_scalar(dst[:, t], src[:, t], mean_var[:, t, 0:1], rstd[:, t:t + 1],
                                            ALU.subtract, ALU.mult).then_inc(d_b, 1)
                return k + t1 - t0

            NORM = 3 * T + 2
            D_X1 = GROUPS + NORM
            D_ROUTE = D_X1 + 1 + 2 * T
            D_PICKS = D_ROUTE + 9
            D_SLOTS = D_PICKS + 14
            D_OWNER = D_SLOTS + 4
            OUT_NORM = 3 * TPC + 2

            @block.sync
            def _(sp):
                sp.dma_start(x_in[:], x_rows).then_inc(x_here, 16)
                for dst, src in ((wg, gate_cols), (wu, up_cols), (wd, down_cols)):
                    sp.dma_start(dst.rearrange("p (e n) -> p e n", e=NE), src).then_inc(wload, 16)

                def get(b, slot, nth):
                    sp.dma_start(x_blk[:, slot], x_slots[bass.ds(b * P, P), :]).then_inc(x_got[slot], 16)

                def step(sp, b, slot, nth):
                    if not (isinstance(b, int) and b + 2 >= BLOCKS):
                        if not is_first(b):
                            sp.wait_ge(x_turned, b)
                        get(b + 2, (slot + 2) % 3, nth)
                    if not is_first(b):
                        put(b - 1, (slot + 2) % 3)

                def put(b, slot):
                    sp.wait_ge(y_kept, b + 2)
                    sp.dma_start(y_slots[bass.ds(b * P, P), :], y_blk[:, slot]).then_inc(y_put[slot], 16)

                sp.wait_ge(scattered, TOP * T * 16)
                get(0, 0, 0)
                get(1, 1, 0)
                block_steps(sp, step)
                put(BLOCKS - 1, (BLOCKS - 1) % 3)
                for g in range(GROUPS):
                    sp.wait_ge(d_b, D_OWNER + (g + 1) * (2 * TPC + OUT_NORM))
                    sp.dma_start(out.rearrange("b (t p) c -> p (b t) c", p=P)[:, g * TPC:(g + 1) * TPC],
                                 res[:, g * TPC:(g + 1) * TPC]).then_inc(stored, 16)
                sp.wait_ge(stored, GROUPS * 16)

            @block.gpsimd
            def _(pool):
                pool.wait_ge(slots_clear, BLOCKS * 16)
                pool.wait_ge(d_b, D_SLOTS)
                for j in range(TOP):
                    for t in range(T):
                        nc.gpsimd.indirect_dma_start(
                            x_slots[:, :], bass.IndirectOffsetOnAxis(ap=slot_u[:, j, t:t + 1], axis=0),
                            x1[:, t], None).then_inc(scattered, 16)
                for slot in range(3):
                    pool.wait_ge(y_put[slot], 16 * (1 + (BLOCKS - slot + 2) // 3))
                for t in range(T):
                    for j in range(TOP):
                        nc.gpsimd.indirect_dma_start(
                            back[:, j, t], None, y_slots[:, :],
                            bass.IndirectOffsetOnAxis(ap=slot_u[:, j, t:t + 1], axis=0)).then_inc(gathered[t // TPC], 16)

            @block.tensor
            def _(pe):
                for t in range(T):
                    last = nc.tensor.transpose(mx_ps[t // 8][:, (t % 8) * P:(t % 8 + 1) * P], attn[:, t], id_f[:])
                    if t % TPC == TPC - 1:
                        last.then_inc(turned, 1)
                pe.wait_ge(later_in, 9 * 16)
                for g in range(GROUPS):
                    pe.wait_ge(turned_d if g % 2 else turned_a, g // 2 + 1)
                    for t in range(g * TPC, (g + 1) * TPC):
                        o = o_bank[g][:, (t % TPC) * P:(t % TPC + 1) * P]
                        nc.tensor.matmul(o, attn_t[:, t * P:(t + 1) * P], wo[:], start=True, stop=False)
                        last = nc.tensor.matmul(o, ones[:], bo_r[:], start=False, stop=True)
                    last.then_inc(projected, 1)
                for g in range(GROUPS):
                    pe.wait_ge(d_b, GROUPS + 2 * T + 2 + TPC * (g + 1))
                    for t in range(g * TPC, (g + 1) * TPC):
                        last = nc.tensor.transpose(mx_ps[t // 8][:, (t % 8) * P:(t % 8 + 1) * P], x1[:, t], id_f[:])
                    last.then_inc(x1_turned, 1)
                for g in range(GROUPS):
                    pe.wait_ge(x1_d if g % 2 else x1_a, g // 2 + 1)
                    for t in range(g * TPC, (g + 1) * TPC):
                        o = s_ps[0][:, t * NE:(t + 1) * NE]
                        nc.tensor.matmul(o, x1_t[:, t * P:(t + 1) * P], rw[:], start=True, stop=False)
                        last = nc.tensor.matmul(o, ones[:], rb_r[:], start=False, stop=True)
                last.then_inc(routed, 1)
                pe.wait_ge(d_b, D_PICKS)
                pe.wait_ge(ones_set, 1)
                flat = picks_b.rearrange("p t e -> p (t e)")
                o = s_ps[1]
                nc.tensor.matmul(o[:, 0:T * NE], before_sb[:], flat, start=True, stop=True)
                for t in range(T - 1):
                    nc.tensor.matmul(o[:, (t + 1) * NE:T * NE], ones_b[:],
                                     picks_b[:, t:t + 1, :].to_broadcast([P, T - 1 - t, NE]),
                                     start=False, stop=True, skip_group_check=True)
                nc.tensor.matmul(pv_ps[0][:, 0:T * NE], ones_b[:], flat, start=True, stop=True).then_inc(ranked, 1)
                pe.wait_ge(d_b, D_OWNER)
                pe.wait_ge(wload, 3 * 16)
                pe.sem_inc(t_kept, 1)
                pe.sem_inc(y_kept, 1)
                for slot in range(3):
                    pe.sem_inc(y_put[slot], 16)

                def turn(b, slot, nth):
                    pe.wait_ge(x_got[slot], nth * 16 + 16)
                    nc.tensor.transpose(xt_ps, x_blk[:, slot], id_f[:]).then_inc(x_turned, 1)

                def finish_hidden(b, slot):
                    pe.wait_ge(hid_done, b + 1)
                    pe.wait_ge(t_kept, b + 1)
                    for f in range(FB):
                        last = nc.tensor.transpose(t_ps[:, f * P:(f + 1) * P], hid[:, slot, f * P:(f + 1) * P], id_f[:])
                    last.then_inc(t_full, 1)

                def down(b, slot, base):
                    pe.wait_ge(t_kept, b + 2)
                    pe.wait_ge(y_kept, b + 1)
                    for f in range(FB):
                        last = nc.tensor.matmul(y_ps, hid_t[:, slot, f * P:(f + 1) * P],
                                                wd[:, bass.ds(base + f * C, C)],
                                                start=(f == 0), stop=(f == FB - 1))
                    last.then_inc(y_full, 1)

                def expert_of(b):
                    return pe.value_load(owner[0:1, bass.ds(b, 1)], min_val=0, max_val=(NE - 1) * FF)

                def step(pe, b, slot, nth):
                    base = expert_of(b)
                    pe.wait_ge(x_kept, b + 1)
                    nc.tensor.matmul(g_ps[:], x_blk_t[:, slot], wg[:, bass.ds(base, FF)],
                                     start=True, stop=True).then_inc(g_full, 1)
                    if not is_last(b):
                        turn(b + 1, (slot + 1) % 3, nth + (slot + 1) // 3)
                    if not is_first(b):
                        finish_hidden(b - 1, (slot + 2) % 3)
                    nc.tensor.matmul(u_ps[:], x_blk_t[:, slot], wu[:, bass.ds(base, FF)],
                                     start=True, stop=True).then_inc(u_full, 1)
                    if not is_first(b):
                        down(b - 1, (slot + 2) % 3, expert_of(b - 1))

                turn(0, 0, 0)
                block_steps(pe, step)
                finish_hidden(BLOCKS - 1, (BLOCKS - 1) % 3)
                down(BLOCKS - 1, (BLOCKS - 1) % 3, expert_of(BLOCKS - 1))

            @block.scalar
            def _(act):
                for g in range(0, GROUPS, 2):
                    act.wait_ge(turned, g + 1)
                    nc.scalar.activation(attn_t[:, g * BANK:(g + 1) * BANK], half_bank[g], ACT.Copy).then_inc(turned_a, 1)
                act.wait_ge(d_b, GROUPS + 2 * T + 1)
                nc.scalar.activation(std[:], std[:], ACT.Sqrt).then_inc(a_b, 1)
                for g in range(0, GROUPS, 2):
                    act.wait_ge(x1_turned, g + 1)
                    nc.scalar.activation(x1_t[:, g * BANK:(g + 1) * BANK], half_bank[g], ACT.Copy).then_inc(x1_a, 1)
                act.wait_ge(d_b, D_ROUTE + 2)
                nc.scalar.activation(e_gap[:], gap[:], ACT.Exp).then_inc(a_b, 1)

                def keep_block(b, slot):
                    act.wait_ge(x_turned, b + 1)
                    nc.scalar.activation(x_blk_t[:, slot], xt_ps, ACT.Copy).then_inc(x_kept, 1)

                def keep_hidden(b, slot):
                    act.wait_ge(t_full, b + 1)
                    nc.scalar.activation(hid_t[:, slot], t_ps[:], ACT.Copy).then_inc(t_kept, 1)

                def step(act, b, slot, nth):
                    act.wait_ge(g_full, b + 1)
                    nc.scalar.activation(sg[:, slot], g_ps[:], ACT.Silu).then_inc(silu_done, 1)
                    if not is_last(b):
                        keep_block(b + 1, (slot + 1) % 3)
                    if not is_first(b):
                        keep_hidden(b - 1, (slot + 2) % 3)

                keep_block(0, 0)
                block_steps(act, step)
                keep_hidden(BLOCKS - 1, (BLOCKS - 1) % 3)
                for g in range(GROUPS):
                    act.wait_ge(d_b, D_OWNER + g * (2 * TPC + OUT_NORM) + 4 * TPC + 1)
                    sl = slice(g * TPC, (g + 1) * TPC)
                    nc.scalar.activation(std[:, sl], std[:, sl], ACT.Sqrt).then_inc(a_b, 1)

            @block.vector
            def _(dve):
                nc.vector.memset(ones_b[:], 1.0).then_inc(ones_set, 1)
                for g in range(1, GROUPS, 2):
                    dve.wait_ge(turned, g + 1)
                    nc.vector.tensor_copy(attn_t[:, g * BANK:(g + 1) * BANK], half_bank[g]).then_inc(turned_d, 1)
                dve.wait_ge(x_here, 16)
                seq = link(dve, d_b, 0)
                for g in range(GROUPS):
                    dve.wait_ge(projected, g + 1)
                    sl = slice(g * TPC, (g + 1) * TPC)
                    nc.vector.tensor_tensor(y[:, sl], o_bank[g].rearrange("p (t c) -> p t c", c=C), x_in[:, sl],
                                            ALU.add).then_inc(d_b, 1)
                dve.wait_ge(d_b, GROUPS)
                k = norm(dve, seq, GROUPS, y, x1, 1)
                for g in range(1, GROUPS, 2):
                    dve.wait_ge(x1_turned, g + 1)
                    nc.vector.tensor_copy(x1_t[:, g * BANK:(g + 1) * BANK], half_bank[g]).then_inc(x1_d, 1)
                dve.wait_ge(routed, 1)
                seq(nc.vector.tensor_copy(logits.rearrange("p t e -> p (t e)"), s_ps[0][:, 0:T * NE]), k + 1)
                k += 1
                for t in range(T):
                    nc.vector.max(top[:, t], logits[:, t]).then_inc(d_b, 1)
                k += T
                dve.wait_ge(d_b, k)
                for t in range(T):
                    nc.vector.max_index(top_id[:, t], top[:, t], logits[:, t]).then_inc(d_b, 1)
                k += T
                dve.wait_ge(d_b, k)
                assert k == D_ROUTE
                seq(nc.vector.tensor_copy(top_f[:], top_id[:, :, 0:2]), k + 1)
                seq(nc.vector.tensor_tensor(gap[:], top[:, :, 1], top[:, :, 0], ALU.subtract), k + 2)
                dve.wait_ge(a_b, 2)
                seq(nc.vector.tensor_scalar(e_sum[:], e_gap[:], 1.0, None, ALU.add), k + 3)
                seq(nc.vector.reciprocal(gate[:, 0], e_sum[:]), k + 4)
                seq(nc.vector.tensor_tensor(gate[:, 1], e_gap[:], gate[:, 0], ALU.mult), k + 5)
                k += 5
                for j in range(2):
                    seq(nc.vector.tensor_tensor(pick[:, j], ids_sb[:].unsqueeze(1).to_broadcast([P, T, NE]),
                                                top_f[:, :, j:j + 1].to_broadcast([P, T, NE]), ALU.is_equal), k + 1)
                    k += 1
                seq(nc.vector.tensor_tensor(picks[:], pick[:, 0], pick[:, 1], ALU.add), k + 1)
                seq(nc.vector.tensor_copy(picks_b[:], picks[:]), k + 2)
                k += 2
                assert k == D_PICKS
                dve.wait_ge(ranked, 1)
                seq(nc.vector.reduce_sum(count[:], pv_ps[0][:, 0:T * NE].rearrange("p (t e) -> p e t", e=NE), AX.X), k + 1)
                seq(nc.vector.tensor_tensor(over[:], count[:].unsqueeze(2).to_broadcast([P, NE, T]),
                                            steps_sb[:].unsqueeze(1).to_broadcast([P, NE, T]), ALU.is_gt), k + 2)
                seq(nc.vector.reduce_sum(n_blocks[:], over[:], AX.X), k + 3)
                seq(nc.vector.tensor_tensor(over8[:], n_blocks[:].unsqueeze(1).to_broadcast([P, NE, NE]),
                                            tri_sb[:].rearrange("p (a b) -> p a b", b=NE), ALU.mult), k + 4)
                seq(nc.vector.reduce_sum(start[:], over8[:], AX.X), k + 5)
                seq(nc.vector.tensor_tensor(stop_at[:], start[:], n_blocks[:], ALU.add), k + 6)
                seq(nc.vector.tensor_scalar(start128[:], start[:], float(P), None, ALU.mult), k + 7)
                seq(nc.vector.tensor_tensor(slot_of[:], s_ps[1][:, 0:T * NE].rearrange("p (t e) -> p t e", e=NE),
                                            start128[:].unsqueeze(1).to_broadcast([P, T, NE]), ALU.add), k + 8)
                k += 8
                for j in range(TOP):
                    seq(nc.vector.tensor_tensor(slot_j[:, j], pick[:, j], slot_of[:], ALU.mult), k + 1)
                    seq(nc.vector.reduce_sum(slot_f[:, j], slot_j[:, j], AX.X), k + 2)
                    seq(nc.vector.tensor_copy(slot_u[:, j], slot_f[:, j]), k + 3)
                    k += 3
                assert k == D_SLOTS
                seq(nc.vector.tensor_tensor(past[:], numbers_sb[:].unsqueeze(2).to_broadcast([1, BLOCKS, NE]),
                                            stop_at[0:1, :].unsqueeze(1).to_broadcast([1, BLOCKS, NE]), ALU.is_ge), k + 1)
                seq(nc.vector.reduce_sum(owner_f[:], past[:], AX.X), k + 2)
                seq(nc.vector.tensor_scalar(owner_g[:], owner_f[:], float(NE - 1), float(FF), ALU.min, ALU.mult), k + 3)
                seq(nc.vector.tensor_copy(owner[:], owner_g[:]), k + 4)
                k += 4
                assert k == D_OWNER

                def keep_result(dve, b, slot, nth):
                    dve.wait_ge(y_full, b + 1)
                    dve.wait_ge(y_put[slot], nth * 16 + 16)
                    nc.vector.tensor_copy(y_blk[:, slot], y_ps).then_inc(y_kept, 1)

                def step(dve, b, slot, nth):
                    dve.wait_ge(silu_done, b + 1)
                    dve.wait_ge(u_full, b + 1)
                    nc.vector.tensor_tensor(hid[:, slot], sg[:, slot], u_ps[:], ALU.mult).then_inc(hid_done, 1)
                    if not is_first(b):
                        keep_result(dve, b - 1, (slot + 2) % 3, nth - (1 if slot == 0 else 0))

                block_steps(dve, step)
                keep_result(dve, BLOCKS - 1, (BLOCKS - 1) % 3, (BLOCKS - 1) // 3)
                for g in range(GROUPS):
                    dve.wait_ge(gathered[g], TOP * TPC * 16)
                    for j, add in ((0, x1), (1, y)):
                        for t in range(g * TPC, (g + 1) * TPC):
                            nc.vector.scalar_tensor_tensor(out=y[:, t], in0=back[:, j, t], scalar=gate[:, j, t:t + 1],
                                                           in1=add[:, t], op0=ALU.mult, op1=ALU.add).then_inc(d_b, 1)
                        k += TPC
                        dve.wait_ge(d_b, k)
                    k = norm(dve, seq, k, y, res, 3 + g, g * TPC, (g + 1) * TPC)


def constants():
    bf = mybir.dt.np(mybir.dt.bfloat16)
    freq = (1.0 / 10000.0 ** (np.arange(0, DK, 2, dtype=np.float32) / np.float32(DK))).astype(np.float32).astype(np.float64)
    pos = np.arange(S, dtype=np.float64)
    ang = freq[:, None] * pos[None, :]
    half = DK // 2
    sin8 = np.concatenate([np.sin(ang), np.sin(ang)])
    cos8 = np.concatenate([np.cos(ang), -np.cos(ang)])
    rot_sin = np.tile(sin8, (NH, 1)).astype(np.float32)
    rot_cos = np.tile(cos8, (NH, 1)).astype(np.float32)

    def parts(a):
        a = a.astype(np.float32)
        hi = a.astype(bf)
        r = a - hi.astype(np.float32)
        mid = r.astype(bf)
        return [hi, mid, (r - mid.astype(np.float32)).astype(bf)]

    def keys(shift):
        g = freq[:, None] * (pos - shift)[None, :]
        e = parts(np.concatenate([np.cos(g), np.sin(g)]))
        return np.concatenate([e[p] for p in K_PARTS])

    one = np.ones((3, S), bf)
    corner_q = np.zeros((CORNERS, S), bf)
    corner_k = np.zeros((CORNERS, S), bf)
    for t in range(CORNERS):
        corner_q[t, t * P + P - 1] = 1
        corner_k[t, (t + 1) * P] = NEG
    q, k = np.arange(P)[:, None], np.arange(P)[None, :]
    mask_low = np.where(k <= q, 0, NEG).astype(bf)
    fold = np.zeros((P, DK + 1), np.float32)
    for p in range(P):
        if p % 32 <= DK:
            fold[p, p % 32] = 1
    last = np.zeros((P, 1), np.float32)
    last[P - 1] = NEG
    return {
        "rot_sin": rot_sin, "rot_cos": rot_cos,
        "k_low_const": np.concatenate([keys(0), one]),
        "k_up_const": np.concatenate([keys(S), corner_k, one]),
        "q_up_const": corner_q,
        "mask_low4": np.tile(mask_low, (1, TPC)),
        "mask_up": np.where(k >= q + 2, 0, NEG).astype(bf),
        "ident_b": np.eye(P).astype(bf), "ident_f": np.eye(P, dtype=np.float32),
        "fold": fold, "last_token": last,
        "expert_ids": np.tile(np.arange(NE, dtype=np.float32), (P, 1)),
        "steps": np.tile(np.arange(T, dtype=np.float32) * P, (P, 1)),
        "triangle": np.tile((np.arange(NE)[None, :] < np.arange(NE)[:, None]).astype(np.float32).reshape(1, -1), (P, 1)),
        "numbers": np.arange(BLOCKS, dtype=np.float32)[None],
        "before": (q < k).astype(np.float32).astype(bf),
    }


def kernel(**inputs):
    import concourse.bacc as bacc
    from concourse.bass_utils import run_bass_kernel_spmd as run

    g = {k[3:]: np.asarray(v) for k, v in inputs.items()}
    wq, wk, wv = g["attn_Wq"], g["attn_Wk"], g["attn_Wv"]
    swap = lambda a: np.roll(a.reshape(a.shape[:-1] + (NH, DK)), DK // 2, axis=-1).reshape(a.shape)
    x = g["attn_x"][0]
    u, v = g["attn_u"].reshape(-1), g["attn_v"].reshape(-1)
    data = {
        "x_rows": x.reshape(T, P, C).transpose(1, 0, 2), "x_cols": x.T,
        "w_qkv": np.stack([wq, swap(wq), wk, wv], axis=1),
        "uv_cols": np.stack([u, v, swap(v)], axis=1), "u_row": u[None],
        "w_o": g["attn_Wo"], "bo_row": g["attn_bo"][None],
        "router_cols": g["ffn_router_w"].T, "router_bias": g["ffn_router_b"][None],
        "gate_cols": g["ffn_gate_w"].transpose(2, 0, 1), "up_cols": g["ffn_up_w"].transpose(2, 0, 1),
        "down_cols": g["ffn_down_w"].transpose(0, 2, 1).reshape(NE, FF // P, P, C).transpose(2, 0, 1, 3).reshape(P, NE, FF),
        **constants(),
    }
    nc = bacc.Bacc("TRN2", target_bir_lowering=False, num_devices=1)
    arrays, args = {}, {}
    for name, a in data.items():
        a = np.ascontiguousarray(a)
        arrays[name] = a
        args[name] = nc.dram_tensor(name, a.shape, mybir.dt.from_np(a.dtype), kind="ExternalInput").ap()
    for name in ("q_scratch", "r_scratch", "k_scratch"):
        args[name] = nc.dram_tensor(name, (NH, 3, DK, S), mybir.dt.bfloat16).ap()
    for name in ("x_slots", "y_slots"):
        args[name] = nc.dram_tensor(name, (BLOCKS * P, C), mybir.dt.float32).ap()
    args["out"] = nc.dram_tensor("out", (1, S, C), mybir.dt.float32, kind="ExternalOutput").ap()
    build(nc, **args)
    r = run(nc, [arrays], core_ids=[0])
    return r.results[0]["out"]
```
